# Optimizing a Trainium2 kernel written in Bass

```python
import numpy as np
import jax
import jax.numpy as jnp

def _softmax(x, axis=-1):
    return jax.nn.softmax(x, axis=axis)

def _gelu(x):
    return jax.nn.gelu(x, approximate=True)

def _silu(x):
    return jax.nn.silu(x)

def _sigmoid(x):
    return jax.nn.sigmoid(x)

def _layernorm(x, axis=-1, eps=1e-05):
    m = jnp.mean(x, axis=axis, keepdims=True)
    v = jnp.var(x, axis=axis, keepdims=True)
    return (x - m) / jnp.sqrt(v + eps)

def _scatter_add(tgt, idx, src, axis=0):
    return tgt.at[idx].add(src)

def _segment_sum(src, seg, n):
    return jax.ops.segment_sum(src, seg, n)
kernel_name = 'mk_gnn_ffn_d1_gnn_r8_c888c3'

def setup_inputs(seed: int=0):
    np.random.seed(seed)
    _w = jnp.asarray

    def _rec_inputs():
        import jax
        import jax.numpy as jnp
        _gk = jax.random.key(seed)
        x = -0.0002117 + 1 * jax.random.normal(jax.random.fold_in(_gk, 1), (6250, 256), jnp.float32)
        src = jax.random.randint(jax.random.fold_in(_gk, 2), (100000,), 0, 6250, jnp.int32)
        dst = jnp.minimum((6250 * jax.random.uniform(jax.random.fold_in(_gk, 3), (100000,)) ** 2.0).astype(jnp.int32), 49999)
        _o = jnp.argsort(dst, stable=True)
        src = src[_o]
        dst = dst[_o]
        return (x, src, dst)
    x, src, dst = _rec_inputs()

    def _L0_gnn_setup():
        import jax, jax.numpy as jnp
        import numpy as np
        N_NODES = 12500
        N_EDGES = 40000
        D_MODEL = 256
        D_Q = D_MODEL // 16
        key = jax.random.key(seed)
        k1, k2, k3, k4 = jax.random.split(key, 4)
        Xe = jax.random.normal(k1, (N_NODES, D_MODEL), dtype=jnp.float32)
        src = jax.random.randint(k2, (N_EDGES,), 0, N_NODES, dtype=jnp.int64)
        dst = jax.random.randint(k3, (N_EDGES,), 0, N_NODES, dtype=jnp.int64)
        W_dis = jax.random.normal(k4, (D_Q, D_MODEL), dtype=jnp.float32) * (1.0 / np.sqrt(D_MODEL))
        return {'Xe': Xe, 'src': src, 'dst': dst, 'W_dis': W_dis}
    _L0_gnn_all = _L0_gnn_setup()
    _L0_gnn_in = {k: v for k, v in _L0_gnn_all.items() if k in ('W_dis',)}
    del _L0_gnn_all

    def _L0_ffn_setup():
        import jax, jax.numpy as jnp
        import numpy as np
        BN_EPS = 0.001

        def _bn(h, g, b, m, v):
            return g * (h - m) * jax.lax.rsqrt(v + BN_EPS) + b
        key = jax.random.key(seed)
        ks = jax.random.split(key, 8)
        B, F, Df = (256, 64, 256)
        E, H, D = (8, 256, 256)
        s1 = 1.0 / np.sqrt(Df)
        s2 = 1.0 / np.sqrt(H)
        return {'x': jax.random.normal(ks[0], (B, F, Df), jnp.float32), 'Wr': jax.random.normal(ks[1], (Df, E), jnp.float32) * s1, 'br': jnp.zeros((E,), jnp.float32), 'W1': jax.random.normal(ks[2], (E, Df, H), jnp.float32) * s1, 'b1': jnp.zeros((E, H), jnp.float32), 'g1': jnp.ones((E, H), jnp.float32), 'be1': jnp.zeros((E, H), jnp.float32), 'm1': jnp.zeros((E, H), jnp.float32), 'v1': jnp.ones((E, H), jnp.float32), 'W2': jax.random.normal(ks[3], (E, H, H), jnp.float32) * s2, 'b2': jnp.zeros((E, H), jnp.float32), 'g2': jnp.ones((E, H), jnp.float32), 'be2': jnp.zeros((E, H), jnp.float32), 'm2': jnp.zeros((E, H), jnp.float32), 'v2': jnp.ones((E, H), jnp.float32), 'Wo': jax.random.normal(ks[4], (E, H, D), jnp.float32) * s2, 'bo': jnp.zeros((E, D), jnp.float32)}
    _L0_ffn_all = _L0_ffn_setup()
    _L0_ffn_in = {k: v for k, v in _L0_ffn_all.items() if k in ('Wr', 'br', 'W1', 'b1', 'g1', 'be1', 'm1', 'v1', 'W2', 'b2', 'g2', 'be2', 'm2', 'v2', 'Wo', 'bo')}
    del _L0_ffn_all
    return {'x': x, 'src': src, 'dst': dst, 'L0_gnn_W_dis': _L0_gnn_in['W_dis'], 'L0_ffn_Wr': _L0_ffn_in['Wr'], 'L0_ffn_br': _L0_ffn_in['br'], 'L0_ffn_W1': _L0_ffn_in['W1'], 'L0_ffn_b1': _L0_ffn_in['b1'], 'L0_ffn_g1': _L0_ffn_in['g1'], 'L0_ffn_be1': _L0_ffn_in['be1'], 'L0_ffn_m1': _L0_ffn_in['m1'], 'L0_ffn_v1': _L0_ffn_in['v1'], 'L0_ffn_W2': _L0_ffn_in['W2'], 'L0_ffn_b2': _L0_ffn_in['b2'], 'L0_ffn_g2': _L0_ffn_in['g2'], 'L0_ffn_be2': _L0_ffn_in['be2'], 'L0_ffn_m2': _L0_ffn_in['m2'], 'L0_ffn_v2': _L0_ffn_in['v2'], 'L0_ffn_Wo': _L0_ffn_in['Wo'], 'L0_ffn_bo': _L0_ffn_in['bo']}

def reference(x, src, dst, L0_gnn_W_dis, L0_ffn_Wr, L0_ffn_br, L0_ffn_W1, L0_ffn_b1, L0_ffn_g1, L0_ffn_be1, L0_ffn_m1, L0_ffn_v1, L0_ffn_W2, L0_ffn_b2, L0_ffn_g2, L0_ffn_be2, L0_ffn_m2, L0_ffn_v2, L0_ffn_Wo, L0_ffn_bo):
    import jax
    import jax.numpy as jnp

    def _L0_gnn_ref(Xe, src, dst, W_dis):
        import jax, jax.numpy as jnp
        import numpy as np
        N_NODES = 12500
        N_EDGES = 40000
        D_MODEL = 256
        D_Q = D_MODEL // 16
        n_nodes = Xe.shape[0]
        q = Xe @ W_dis.T * 0.25
        E = jnp.sum(q[src] * q[dst], axis=-1)
        aij = jax.nn.relu(E)
        rij = jax.nn.relu(-E)
        A_sum = jax.ops.segment_sum(aij, dst, num_segments=n_nodes)
        R_sum = jax.ops.segment_sum(rij, dst, num_segments=n_nodes)
        XeA_sum = jax.ops.segment_sum(Xe[src] * aij[:, None], dst, num_segments=n_nodes)
        denom = A_sum + R_sum + 0.01
        Xe_trans = (XeA_sum + Xe * R_sum[:, None]) / denom[:, None]
        return Xe_trans

    def _L0_ffn_ref(x, Wr, br, W1, b1, g1, be1, m1, v1, W2, b2, g2, be2, m2, v2, Wo, bo):
        import jax, jax.numpy as jnp
        import numpy as np
        BN_EPS = 0.001

        def _bn(h, g, b, m, v):
            return g * (h - m) * jax.lax.rsqrt(v + BN_EPS) + b
        feat = jnp.mean(x, axis=0)
        w = jax.nn.softmax(feat @ Wr + br, axis=-1)
        h = jnp.einsum('bfd,edh->bfeh', x, W1) + b1
        h = jax.nn.relu(_bn(h, g1, be1, m1, v1))
        h = jnp.einsum('bfeh,ehk->bfek', h, W2) + b2
        h = jax.nn.relu(_bn(h, g2, be2, m2, v2))
        y = jnp.einsum('bfeh,ehd->bfed', h, Wo) + bo
        return jnp.einsum('bfed,fe->bfd', y, w)
    x = x + _L0_gnn_ref(_layernorm(x, axis=-1), src, dst, L0_gnn_W_dis)
    x = x + _L0_ffn_ref(_layernorm(x, axis=-1)[None], L0_ffn_Wr, L0_ffn_br, L0_ffn_W1, L0_ffn_b1, L0_ffn_g1, L0_ffn_be1, L0_ffn_m1, L0_ffn_v1, L0_ffn_W2, L0_ffn_b2, L0_ffn_g2, L0_ffn_be2, L0_ffn_m2, L0_ffn_v2, L0_ffn_Wo, L0_ffn_bo)[0]
    return x

_drawn_inputs = setup_inputs


def setup_inputs(seed=0):
    import zlib

    import numpy as np

    out = dict(_drawn_inputs(seed))
    spreads = {'L0_ffn_br': (0.0, 0.36),
     'L0_ffn_b1': (0.0, 0.481),
     'L0_ffn_g1': (1.0, 0.2),
     'L0_ffn_be1': (0.0, 0.491),
     'L0_ffn_m1': (0.0, 0.479),
     'L0_ffn_v1': (1.0, 0.6),
     'L0_ffn_b2': (0.0, 0.343),
     'L0_ffn_g2': (1.0, 0.2),
     'L0_ffn_be2': (0.0, 0.359),
     'L0_ffn_m2': (0.0, 0.354),
     'L0_ffn_v2': (1.0, 0.6),
     'L0_ffn_bo': (0.0, 0.1)}
    factors = {}
    for name, (base, spread) in spreads.items():
        noise = np.random.default_rng([zlib.crc32(name.encode()), seed]).standard_normal(out[name].shape)
        drawn = base * np.exp(spread * noise) if base else spread * noise
        out[name] = jnp.asarray(drawn.astype(out[name].dtype))
    for name, factor in factors.items():
        out[name] = (out[name] * factor).astype(out[name].dtype)
    return out
```

```python
from contextlib import ExitStack

import concourse.bass as bass
from concourse import mybir
from concourse.alu_op_type import AluOpType as ALU

ACT = mybir.ActivationFunctionType
AX = mybir.AxisListType
F32 = mybir.dt.float32
F32R = mybir.dt.float32r
BF16 = mybir.dt.bfloat16
I32 = mybir.dt.int32
DVE_ENGINE = mybir.EngineType.DVE
PE_ENGINE = mybir.EngineType.PE

P = 128


def graph_mixture(nc, x, src, dst, w_dis, wr, br, bn1, bn2, w1, w2, wo, bo, out):
    N, D = x.shape
    E = src.shape[0]
    Q = w_dis.shape[0]
    NE = wr.shape[1]
    KC = D // P
    NB = -(-N // P)
    TAIL = N - (NB - 1) * P
    NT = -(-E // P)
    TC = -(-NT // P)
    FULL = (TC - 1) * P
    LAST = NT - 1 - FULL
    ETAIL = E - (NT - 1) * P
    SB = 8
    UN = 2
    STEPS = -(-(NT + NB - 1) // (SB * UN)) * SB * UN
    NBATCH = STEPS // SB
    SH = STEPS // 2
    ROW = D + Q
    MW = D + 2
    LN_EPS, BN_EPS, DEN_EPS = 1e-5, 1e-3, 0.01
    PAD = float(1 << 20)
    GB = 3
    NG = -(-NB // GB)
    TOK = GB * P
    LC = 8
    CH = (NB - 1) // LC
    assert SH <= 512 and NB - (NG - 1) * GB == 1 and (NB - 1) % (2 * LC) == 0

    xn_table = nc.dram_tensor("xn_table", [NB * P, ROW], F32)
    dst_rows = nc.dram_tensor("dst_rows", [NBATCH, SB * P], BF16)
    gate_rows = nc.dram_tensor("gate_rows", [NE, NB * P + 2 * P], F32)
    table_ap, rows_ap, gates_ap = xn_table.ap(), dst_rows.ap(), gate_rows.ap()

    top, graph = ExitStack(), ExitStack()
    with top:
        def sem(name):
            return top.enter_context(nc.semaphore(name))

        def sb(ctx, name, shape, dt):
            return ctx.enter_context(nc.sbuf_tensor(name, shape, dt, side="right" if ctx is graph else "left"))

        bank = [top.enter_context(nc.psum_tensor(f"bank{i}", [P, 512], F32)) for i in range(8)]

        wh = sb(top, "wh", [P, 3 * NE, KC * D], F32R)
        wl = sb(top, "wl", [P, 3 * NE, KC * D], F32R)
        ident = sb(top, "ident", [P, P], F32)
        bn_s = sb(top, "bn_s", [P, 2, 2 * NE], F32)
        bn_c = sb(top, "bn_c", [P, 2, 2 * NE], F32)
        wr_sb = sb(top, "wr_sb", [P, KC, NE], F32)
        br_sb = sb(top, "br_sb", [P, NE], F32)
        bo_sb = sb(top, "bo_sb", [NE, D], F32)

        top.enter_context(graph)
        src_step = sb(graph, "src_step", [P, NBATCH, SB], I32)
        dst_step = sb(graph, "dst_step", [P, NBATCH, SB], F32)
        q_parts = sb(graph, "q_parts", [P, NB * 3 * Q], BF16)
        at = sb(graph, "at", [P, NBATCH, SB], I32)
        acc_at, q_at = at[0:1], at[32:33]
        iota = sb(graph, "iota", [P, P], F32)
        lane = sb(graph, "lane", [P, 1], F32)

        with ExitStack() as pa:
            x_tile = sb(pa, "x_tile", [P, 2, LC, D], F32)
            xnq = sb(pa, "xnq", [P, 2, LC, ROW], F32)
            raw = sb(pa, "raw", [P, 2, KC * D], F32)
            iota_s = sb(pa, "iota_s", [P, STEPS], F32)
            ones = sb(pa, "ones", [P, P], F32)
            tri = sb(pa, "tri", [P, P], F32)
            dst_i = sb(pa, "dst_i", [P, TC, P], I32)
            src_i = sb(pa, "src_i", [P, TC, P], I32)
            dst_f = sb(pa, "dst_f", [P, TC, P], F32)
            src_f = sb(pa, "src_f", [P, TC, P], F32)
            blk_i = sb(pa, "blk_i", [P, 2, TC], I32)
            blk_j = sb(pa, "blk_j", [P, 2, TC], I32)
            blk_f = sb(pa, "blk_f", [P, 2, TC], F32)
            npair = sb(pa, "npair", [P, TC], F32)
            pref = sb(pa, "pref", [P, 2, TC], F32)
            scan = sb(pa, "scan", [P, TC], F32)
            zero = sb(pa, "zero", [P, TC], F32)
            t_st = sb(pa, "t_st", [P, TC], F32)
            t_en = sb(pa, "t_en", [P, TC], F32)
            t_fs = sb(pa, "t_fs", [P, TC], F32)
            t_fm = sb(pa, "t_fm", [P, TC], F32)
            below = sb(pa, "below", [P, STEPS], F32)
            sel = sb(pa, "sel", [P, STEPS], F32)
            dclamp = sb(pa, "dclamp", [P, TC * P], F32)
            dpos = dclamp[:].rearrange("p (c e) -> p c e", e=P)
            rows_sb = sb(pa, "rows_sb", [P, TC, P], BF16)
            wd_in = sb(pa, "wd_in", [Q, D], F32)
            wd_t = sb(pa, "wd_t", [P, KC, Q], F32)
            par_in = [t[0:2 * NE, n, :].bitcast(F32) for t in (dst_i, src_i) for n in range(5)]
            par = sb(pa, "par", [P, 10, 2 * NE], F32)
            xt = sb(pa, "xt", [P, 2, KC * P], F32)
            stats = sb(pa, "stats", [P, LC, 6], F32)
            mv = sb(pa, "mv", [P, LC, 2], F32)
            var = sb(pa, "var", [P, LC], F32)
            sd = sb(pa, "sd", [P, LC], F32)
            rstd = sb(pa, "rstd", [P, LC], F32)
            qr = sb(pa, "qr", [P, LC * Q], F32)
            qr2 = sb(pa, "qr2", [P, LC * Q], F32)
            bn_v = sb(pa, "bn_v", [P, 2, 2 * NE], F32)
            bn_d = sb(pa, "bn_d", [P, 2, 2 * NE], F32)

            edges_in, small_in, x_in = sem("edges_in"), sem("small_in"), [sem("x_in0"), sem("x_in1")]
            tail_cleared = sem("tail_cleared")
            raw_in = [sem("raw_in0"), sem("raw_in1")]
            hi_done, lo_done = sem("hi_done"), sem("lo_done")
            cleared, consts = sem("cleared"), sem("consts")
            dve_a, act_a, pool_a = sem("dve_a"), sem("act_a"), sem("pool_a")
            n_ready, pref_done = sem("n_ready"), sem("pref_done")
            dprime, sel_ready, sel_used = sem("dprime"), sem("sel_ready"), sem("sel_used")
            evac, rowt_done, rowt_copied, rows_out = sem("evac"), sem("rowt_done"), sem("rowt_copied"), sem("rows_out")
            part_done, bn_var, bn_sd = sem("part_done"), sem("bn_var"), sem("bn_sd")
            var_ready, sd_ready, xn_ready = sem("var_ready"), sem("sd_ready"), sem("xn_ready")
            xt_done, xt_copied, q_done, q_copied = sem("xt_done"), sem("xt_copied"), sem("q_done"), sem("q_copied")
            table_out, xnq_free = [sem("table_out0"), sem("table_out1")], sem("xnq_free")

            def chunks(eng, body, before_last=None):
                with eng.Fori(0, CH // 2) as it:
                    body(it * 2, LC, 0)
                    body(it * 2 + 1, LC, 1)
                if before_last:
                    before_last()
                body(CH, 1, 0)

            block = pa.enter_context(nc.Block())

            @block.sync
            def _(sp):
                sp.wait_ge(cleared, 2)
                for a, t in ((dst, dst_i), (src, src_i)):
                    sp.dma_start(t[:, 0:TC - 1, :], a[0:FULL * P].rearrange("(c p e) -> p c e", p=P, e=P)).then_inc(edges_in, 16)
                    sp.dma_start(t[0:LAST, TC - 1, :], a[FULL * P:(NT - 1) * P].rearrange("(p e) -> p e", e=P)).then_inc(edges_in, 16)
                    sp.dma_start(t[LAST:LAST + 1, TC - 1, 0:ETAIL], a[(NT - 1) * P:E].rearrange("(p e) -> p e", p=1)).then_inc(edges_in, 16)
                sp.dma_start(wd_in[:], w_dis).then_inc(small_in, 16)
                sp.dma_start(wr_sb[:], wr.rearrange("(k p) e -> p k e", p=P)).then_inc(small_in, 16)
                sp.dma_start(br_sb[:], br.partition_broadcast(P)).then_inc(small_in, 16)
                sp.dma_start(bo_sb[:], bo).then_inc(small_in, 16)

                def load_x(c, par):
                    sp.dma_start(x_tile[:, par], x[bass.ds(c * (LC * P), LC * P), :].rearrange("(b p) d -> p b d", p=P)).then_inc(x_in[par], 16)

                load_x(0, 0)
                load_x(1, 1)
                sp.wait_ge(n_ready, 1)
                for n, a in enumerate((*bn1, *bn2)):
                    sp.dma_start(par_in[n], a.rearrange("e (m p) -> (e m) p", p=P)).then_inc(small_in, 16)
                for layer, w in enumerate((w1, w2, wo)):
                    for e in range(NE):
                        n = layer * NE + e
                        if n >= 2:
                            sp.wait_ge(lo_done, n - 1)
                        sp.dma_start(raw[:, n % 2, :].rearrange("p (k h) -> p k h", k=KC),
                                     w[e].rearrange("(k p) h -> p k h", p=P)).then_inc(raw_in[n % 2], 16)
                with sp.Fori(1, CH // 2) as it:
                    for par_ in range(2):
                        sp.wait_ge(xn_ready, it * 2 + par_ - 1)
                        load_x(it * 2 + par_, par_)
                sp.wait_ge(xn_ready, CH - 1)
                sp.wait_ge(tail_cleared, 1)
                sp.dma_start(x_tile[0:TAIL, 0, 0, :], x[(NB - 1) * P:N, :]).then_inc(x_in[0], 16)
                sp.wait_ge(rowt_copied, TC)
                flat = rows_ap.rearrange("k (s e) -> (k s) e", e=P)
                whole = STEPS // P
                sp.dma_start(flat[0:whole * P, :].rearrange("(c p) e -> p c e", p=P), rows_sb[:, 0:whole, :]).then_inc(rows_out, 16)
                sp.dma_start(flat[whole * P:STEPS, :], rows_sb[0:STEPS - whole * P, whole, :]).then_inc(rows_out, 16)
                sp.wait_ge(rows_out, 32)

            @block.gpsimd
            def _(pool):
                pool.sem_inc(xnq_free, 2)
                nc.gpsimd.memset(dst_i[:, TC - 1, :], -int(PAD)).then_inc(cleared, 1)
                nc.gpsimd.memset(src_i[:, TC - 1, :], 0).then_inc(cleared, 1)
                nc.gpsimd.memset(ones[:], 1.0).then_inc(pool_a, 1)
                nc.gpsimd.memset(zero[:], 0.0).then_inc(pool_a, 1)
                pool.wait_ge(pool_a, 1)
                nc.gpsimd.affine_select(out=ident[:], in_=ones[:], compare_op=ALU.is_equal, fill=0.0, base=0,
                                        pattern=[[-1, P]], channel_multiplier=1).then_inc(consts, 1)
                nc.gpsimd.affine_select(out=tri[:], in_=ones[:], compare_op=ALU.is_gt, fill=0.0, base=0,
                                        pattern=[[1, P]], channel_multiplier=-1).then_inc(consts, 1)
                nc.gpsimd.iota(iota_s[:], pattern=[[1, STEPS]], base=0, channel_multiplier=0,
                               allow_small_or_imprecise_dtypes=True).then_inc(consts, 1)
                nc.gpsimd.iota(iota[:], pattern=[[1, P]], base=0, channel_multiplier=0,
                               allow_small_or_imprecise_dtypes=True).then_inc(consts, 1)
                nc.gpsimd.iota(lane[:], pattern=[[0, 1]], base=0, channel_multiplier=1,
                               allow_small_or_imprecise_dtypes=True).then_inc(consts, 1)
                for n in range(3 * NE):
                    pool.wait_ge(hi_done, n + 1)
                    nc.gpsimd.tensor_tensor(out=wl[:, n, :], in0=raw[:, n % 2, :], in1=wh[:, n, :].bitcast(F32),
                                            op=ALU.subtract).then_inc(lo_done, 1)

                def body(c, nb, par_):
                    pool.wait_ge(q_copied, c + 1)
                    pool.dma_start(table_ap[bass.ds(c * (LC * P), nb * P), :].rearrange("(b p) r -> p b r", p=P),
                                   xnq[:, par_, 0:nb, :]).then_inc(table_out[par_], 16)
                    pool.wait_ge(table_out[par_], (c - par_) * 8 + 16)
                    pool.sem_inc(xnq_free, 1)

                chunks(pool, body, lambda: [
                    pool.wait_ge(xn_ready, CH - 1),
                    nc.gpsimd.memset(x_tile[:, 0, 0, :], 0.0).then_inc(tail_cleared, 1)])

            @block.scalar
            def _(act):
                for n in range(3 * NE):
                    act.wait_ge(raw_in[n % 2], 16 * (n // 2 + 1))
                    nc.scalar.copy(wh[:, n, :], raw[:, n % 2, :]).then_inc(hi_done, 1)
                act.wait_ge(bn_var, 1)
                nc.scalar.activation(bn_d[:], bn_v[:], ACT.Sqrt).then_inc(bn_sd, 1)

                def body(c, nb, par_):
                    act.wait_ge(var_ready, c + 1)
                    nc.scalar.activation(sd[:, 0:nb], var[:, 0:nb], ACT.Sqrt).then_inc(sd_ready, 1)
                    for j in range(nb):
                        act.wait_ge(xt_done, c * LC + j + 1)
                        nc.scalar.copy(xt[:, j % 2, :], bank[j % 2][:, 0:KC * P]).then_inc(xt_copied, 1)
                    act.wait_ge(q_done, c * LC + nb)
                    nc.scalar.mul(xnq[:, par_, 0:nb, D:ROW], bank[2][:, 0:nb * Q].rearrange("p (b q) -> p b q", q=Q), 0.25).then_inc(q_copied, 1)

                chunks(act, body)

            @block.tensor
            def _(pe):
                pe.wait_ge(consts, 2)
                pe.wait_ge(n_ready, 1)
                nc.tensor.matmul(bank[6][:, 0:TC], tri[:], npair[:], start=True, stop=True)
                nc.tensor.matmul(bank[6][:, TC:2 * TC], ones[:], npair[:], start=True, stop=True).then_inc(pref_done, 1)
                pe.wait_ge(dprime, 1)
                for c in range(TC):
                    pe.wait_ge(sel_ready, c + 1)
                    for n, lhs in enumerate((src_f[:, c, :], dst_f[:, c, :], t_fs[:, c:c + 1].broadcast_to([P, P]))):
                        for h in range(2):
                            mm = nc.tensor.matmul(bank[2 * n + h][:, 0:SH], lhs, sel[:, h * SH:(h + 1) * SH],
                                                  start=(c == 0), stop=(c == TC - 1))
                    mm.then_inc(sel_used, 1)
                pe.wait_ge(small_in, 16 * 14)
                for n in range(10):
                    nc.tensor.transpose(bank[7][:, n * 2 * NE:(n + 1) * 2 * NE], par_in[n], ident[0:2 * NE, 0:2 * NE])
                for k in range(KC):
                    mm = nc.tensor.transpose(bank[7][:, 160 + k * Q:160 + (k + 1) * Q], wd_in[:, k * P:(k + 1) * P], ident[0:Q, 0:Q])
                mm.then_inc(part_done, 1)
                pe.wait_ge(evac, 1)
                for c in range(TC):
                    if c >= 2:
                        pe.wait_ge(rowt_copied, c - 1)
                    else:
                        pe.wait_ge(bn_var, 1)
                    nc.tensor.transpose(bank[6 + c % 2][:, 0:P], dclamp[:, c * P:(c + 1) * P], ident[:]).then_inc(rowt_done, 1)
                def body(c, nb, par_):
                    pe.wait_ge(xn_ready, c + 1)
                    for j in range(nb + 1):
                        if j < nb:
                            if j >= 2:
                                pe.wait_ge(xt_copied, c * LC + j - 1)
                            for k in range(KC):
                                mm = nc.tensor.transpose(bank[j % 2][:, k * P:(k + 1) * P], xnq[:, par_, j, k * P:(k + 1) * P], ident[:])
                            mm.then_inc(xt_done, 1)
                        if j >= 1:
                            pe.wait_ge(xt_copied, c * LC + j)
                            for k in range(KC):
                                mm = nc.tensor.matmul(bank[2][:, (j - 1) * Q:j * Q], xt[:, (j - 1) % 2, k * P:(k + 1) * P], wd_t[:, k, :],
                                                      start=(k == 0), stop=(k == KC - 1))
                            mm.then_inc(q_done, 1)

                chunks(pe, body)

            @block.vector
            def _(dve):
                done = [0]

                def link(ins):
                    done[0] += 1
                    ins.then_inc(dve_a, 1)
                    dve.wait_ge(dve_a, done[0])

                V = nc.vector
                dve.wait_ge(edges_in, 96)
                V.tensor_copy(dst_f[:], dst_i[:])
                link(V.tensor_copy(src_f[:], src_i[:]))
                link(V.tensor_scalar(dpos, dst_f[:], 0.0, 2 * PAD, ALU.is_lt, ALU.mult))
                link(V.tensor_tensor(dpos, dpos, dst_f[:], ALU.add))
                V.tensor_reduce(blk_i[:, 0, :], dpos, AX.X, ALU.min)
                link(V.tensor_reduce(blk_i[:, 1, :], dst_f[:], AX.X, ALU.max))
                link(V.tensor_scalar(blk_j[:], blk_i[:], 7, None, ALU.arith_shift_right))
                link(V.tensor_copy(blk_f[:], blk_j[:]))
                link(V.tensor_scalar(blk_f[:, 1, :], blk_f[:, 1, :], -1.0, 1.0, ALU.max, ALU.add))
                link(V.tensor_tensor(npair[:], blk_f[:, 1, :], blk_f[:, 0, :], ALU.subtract))
                V.tensor_scalar(npair[:], npair[:], 0.0, None, ALU.max).then_inc(n_ready, 1)
                dve.wait_ge(pref_done, 1)
                dve.wait_ge(pool_a, 2)
                link(V.tensor_copy(pref[:].rearrange("p a c -> p (a c)"), bank[6][:, 0:2 * TC]))
                link(V.tensor_tensor_scan(scan[:], pref[:, 1, :], zero[:], 0.0, ALU.add, ALU.add))
                link(V.tensor_tensor(scan[:], scan[:], pref[:, 1, :], ALU.subtract))
                link(V.tensor_tensor(t_st[:], scan[:], pref[:, 0, :], ALU.add))
                V.tensor_tensor(t_en[:], t_st[:], npair[:], ALU.add)
                link(V.tensor_tensor(t_fs[:], blk_f[:, 0, :], t_st[:], ALU.subtract))
                link(V.tensor_scalar(t_fm[:], t_fs[:], -float(P), None, ALU.mult))
                for c in range(TC):
                    last = V.tensor_scalar(dst_f[:, c, :], dst_f[:, c, :], t_fm[:, c:c + 1], None, ALU.add)
                last.then_inc(dprime, 1)
                dve.wait_ge(consts, 5)
                for c in range(TC):
                    if c >= 1:
                        dve.wait_ge(sel_ready, c)
                    link(V.tensor_scalar(below[:], iota_s[:], t_en[:, c:c + 1], None, ALU.is_lt))
                    if c >= 1:
                        dve.wait_ge(sel_used, c)
                    V.scalar_tensor_tensor(out=sel[:], in0=iota_s[:], scalar=t_st[:, c:c + 1], in1=below[:],
                                           op0=ALU.is_ge, op1=ALU.mult).then_inc(sel_ready, 1)
                dve.wait_ge(sel_used, TC)
                srcv, dstv = (t[:].rearrange("p k s -> p (k s)") for t in (src_step, dst_step))
                atall = at[:].rearrange("p k s -> p (k s)")
                for h in range(2):
                    cols = slice(h * SH, (h + 1) * SH)
                    V.tensor_copy(srcv[:, cols], bank[0 + h][:, 0:SH])
                    V.scalar_tensor_tensor(out=dstv[:, cols], in0=iota_s[:, cols], scalar=-float(P), in1=bank[2 + h][:, 0:SH],
                                           op0=ALU.mult, op1=ALU.add)
                    link(V.tensor_tensor(below[:, cols], iota_s[:, cols], bank[4 + h][:, 0:SH], ALU.add))
                V.tensor_scalar(atall[0:1, :], below[0:1, :], float(NB - 1), float(MW), ALU.min, ALU.mult)
                V.tensor_scalar(atall[32:33, :], below[32:33, :], float(NB - 1), float(3 * Q), ALU.min, ALU.mult)
                V.memset(dclamp[:, STEPS:], -1.0)
                V.tensor_scalar(dclamp[:, 0:STEPS], dstv, -1.0, float(P), ALU.max, ALU.min).then_inc(evac, 1)
                dve.wait_ge(part_done, 1)
                V.tensor_copy(par[:].rearrange("p a b -> p (a b)"), bank[7][:, 0:160])
                link(V.tensor_copy(wd_t[:].rearrange("p k q -> p (k q)"), bank[7][:, 160:160 + KC * Q]))
                pv = par[:].rearrange("p (l n) m -> p l n m", l=2)
                V.tensor_scalar(bn_v[:], pv[:, :, 4, :], BN_EPS, None, ALU.add).then_inc(bn_var, 1)
                for c in range(TC):
                    dve.wait_ge(rowt_done, c + 1)
                    V.tensor_copy(rows_sb[:, c, :], bank[6 + c % 2][:, 0:P]).then_inc(rowt_copied, 1)
                per = 8
                base = done[0]
                here = [0, 0]

                def link_c(ins):
                    here[1] += 1
                    ins.then_inc(dve_a, 1)
                    dve.wait_ge(dve_a, here[0] + here[1])

                def body(c, nb, par_):
                    here[0], here[1] = c * per + base, 0
                    dve.wait_ge(x_in[par_], (c - par_) * 8 + 16)
                    for j in range(nb):
                        last = V.bn_stats(stats[:, j, :], x_tile[:, par_, j, :])
                    link_c(last)
                    V.memset(scan[:, 0:1], 0.0)
                    for j in range(nb):
                        last = V.bn_aggr(mv[:, j, :], stats[:, j, :])
                    link_c(last)
                    V.tensor_scalar(var[:, 0:nb], mv[:, 0:nb, 1], LN_EPS, None, ALU.add).then_inc(var_ready, 1)
                    dve.wait_ge(sd_ready, c + 1)
                    link_c(V.reciprocal(rstd[:, 0:nb], sd[:, 0:nb]))
                    dve.wait_ge(xnq_free, c + 1)
                    for j in range(nb):
                        last = V.tensor_scalar(xnq[:, par_, j, 0:D], x_tile[:, par_, j, :], mv[:, j, 0:1], rstd[:, j:j + 1], ALU.subtract, ALU.mult)
                    last.then_inc(xn_ready, 1)
                    dve.wait_ge(q_copied, c + 1)
                    qv = xnq[:, par_, 0:nb, D:ROW]
                    qp = q_parts[:, bass.ds(c * (LC * 3 * Q), nb * 3 * Q)].rearrange("p (b t q) -> p b t q", t=3, q=Q)
                    q1 = qr[:, 0:nb * Q].rearrange("p (b q) -> p b q", q=Q)
                    q2 = qr2[:, 0:nb * Q].rearrange("p (b q) -> p b q", q=Q)
                    link_c(V.tensor_copy(qp[:, :, 0, :], qv))
                    link_c(V.tensor_tensor(q1, qv, qp[:, :, 0, :], ALU.subtract))
                    link_c(V.tensor_copy(qp[:, :, 1, :], q1))
                    link_c(V.tensor_tensor(q2, q1, qp[:, :, 1, :], ALU.subtract))
                    link_c(V.tensor_copy(qp[:, :, 2, :], q2))
                    assert here[1] == per, here

                chunks(dve, body)
                base += per * (CH + 1)
                dve.wait_ge(bn_sd, 1)
                link2 = [0]

                def link_e(ins):
                    link2[0] += 1
                    ins.then_inc(dve_a, 1)
                    dve.wait_ge(dve_a, base + link2[0])

                link_e(V.reciprocal(bn_v[:], bn_d[:]))
                link_e(V.tensor_tensor(bn_s[:], pv[:, :, 1, :], bn_v[:], ALU.mult))
                link_e(V.tensor_tensor(bn_c[:], pv[:, :, 0, :], pv[:, :, 3, :], ALU.subtract))
                link_e(V.tensor_tensor(bn_c[:], bn_c[:], bn_s[:], ALU.mult))
                V.tensor_tensor(bn_c[:], bn_c[:], pv[:, :, 2, :], ALU.add)


        acc = sb(top, "acc", [P, NB * MW], F32)

        with ExitStack() as pb:
            rows = sb(pb, "rows", [P, UN * SB * ROW], F32)
            index = sb(pb, "index", [P, UN, SB], I32)
            hot_t = sb(pb, "hot_t", [P, UN, SB * P], BF16)
            hot = sb(pb, "hot", [P, UN, SB, P], F32)
            e_sc = sb(pb, "e_sc", [P, UN, SB], F32)
            msg = sb(pb, "msg", [P, UN, SB, MW], F32)
            rowsv = rows[:].rearrange("p (u s r) -> p u s r", u=UN, s=SB)

            index_ready, gathered = sem("index_ready"), [sem(f"gathered{u}") for u in range(UN)]
            index_used, bc_in = sem("index_used"), [sem(f"bc_in{u}") for u in range(UN)]
            hot_t_ready, qd_done, weights_ready = sem("hot_t_ready"), sem("qd_done"), sem("weights_ready")
            hot_ready, msg_ready, product, added = sem("hot_ready"), sem("msg_ready"), sem("product"), sem("added")
            gather_turn, cleared_b, dve_b, scaled = sem("gather_turn"), sem("cleared_b"), sem("dve_b"), sem("scaled")
            ITERS = NBATCH // UN
            block = pb.enter_context(nc.Block())

            @block.sync
            def _(sp):
                with sp.Fori(0, ITERS) as it:
                    for u in range(UN):
                        k = it * UN + u
                        sp.wait_ge(qd_done, k + 1)
                        sp.dma_start(hot_t[:, u, :], rows_ap[bass.ds(k, 1), :].rearrange("a e -> (a e)").partition_broadcast(P)
                                     ).then_inc(bc_in[u], 16)

            @block.gpsimd
            def _(pool):
                with pool.Fori(0, ITERS) as it:
                    for u in range(UN):
                        k = it * UN + u
                        pool.wait_ge(scaled, k + 1)
                        nc.gpsimd.tensor_copy(index[:, u, :], src_step[:, bass.ds(k, 1), :].rearrange("p k s -> p (k s)")).then_inc(index_ready, 1)
                        pool.wait_ge(index_ready, k + 1)
                        pool.sem_inc(gather_turn, 1)
                        for s in range(SB):
                            pool.indirect_dma_start(out=rowsv[:, u, s, :], out_offset=None, in_=table_ap,
                                                    in_offset=bass.IndirectOffsetOnAxis(ap=index[:, u, s:s + 1], axis=0)).then_inc(gathered[u], 16)

            @block.tensor
            def _(pe):
                def q_of_destinations(k, u):
                    pe.wait_ge(hot_t_ready, k + 1)
                    pe.wait_ge(weights_ready, k + 1)
                    _, at = nc.values_load_multi_w_load_instructions(
                        q_at[:, bass.ds(k, 1), :].rearrange("p k s -> p (k s)"), engines=(PE_ENGINE,), min_val=0,
                        max_val=(NB - 1) * 3 * Q, skip_runtime_bounds_check_because="the block was clamped to NB - 1")
                    for s in range(SB):
                        mm = nc.tensor.matmul(bank[6 + u][:, s * 3 * Q:(s + 1) * 3 * Q], hot_t[:, u, s * P:(s + 1) * P],
                                              q_parts[:, bass.ds(at[s], 3 * Q)], start=True, stop=True)
                    mm.then_inc(qd_done, 1)

                pe.sem_inc(qd_done, UN)
                with pe.Fori(0, ITERS) as it:
                    for u in range(UN):
                        k = it * UN + u
                        q_of_destinations(k, u)
                        pe.wait_ge(hot_ready, k + 1)
                        for s in range(SB):
                            pe.wait_ge(msg_ready, k * SB + s + 1)
                            pe.wait_ge(added, k * SB + s + 1)
                            nc.tensor.matmul(bank[s % 4][:, 0:MW], hot[:, u, s, :], msg[:, u, s, :],
                                             start=True, stop=True).then_inc(product, 1)

            @block.scalar
            def _(act):
                act.sem_inc(scaled, UN)
                with act.Fori(0, ITERS) as it:
                    for u in range(UN):
                        k = it * UN + u
                        act.wait_ge(weights_ready, k + 1 + UN)
                        act.wait_ge(gathered[u], (it + 1) * (16 * SB))
                        for s in range(SB):
                            last = nc.scalar.activation(msg[:, u, s, 0:D], rowsv[:, u, s, 0:D], ACT.Copy,
                                                        scale=msg[:, u, s, D:D + 1]).then_inc(msg_ready, 1)
                        act.wait_ge(msg_ready, k * SB + SB)
                        act.sem_inc(scaled, 1)

            @block.vector
            def _(dve):
                V = nc.vector
                dve.sem_inc(weights_ready, UN)
                dve.sem_inc(added, 4)
                V.memset(acc[:], 0.0).then_inc(cleared_b, 1)
                dve.wait_ge(cleared_b, 1)
                PER = 2 * UN
                with dve.Fori(0, ITERS) as it:
                    here = [0]

                    def link(ins):
                        here[0] += 1
                        ins.then_inc(dve_b, 1)
                        dve.wait_ge(dve_b, it * PER + here[0])

                    for u in range(UN):
                        k = it * UN + u
                        dve.wait_ge(bc_in[u], (it + 1) * 16)
                        V.tensor_scalar(hot_t[:, u, :], hot_t[:, u, :], lane[:], None, ALU.is_equal).then_inc(hot_t_ready, 1)
                        V.tensor_tensor(hot[:, u], iota[:].unsqueeze(1).broadcast_to([P, SB, P]),
                                        dst_step[:, bass.ds(k, 1), :].rearrange("p k s -> p (k s)").unsqueeze(2).broadcast_to([P, SB, P]),
                                        ALU.is_equal).then_inc(hot_ready, 1)
                        dve.wait_ge(qd_done, k + 1 + UN)
                        dve.wait_ge(gathered[u], (it + 1) * (16 * SB))
                        qq = msg[:, u, :, 0:3 * Q]
                        link(V.tensor_tensor(qq.rearrange("p s (t q) -> p s t q", t=3),
                                             bank[6 + u][:, 0:SB * 3 * Q].rearrange("p (s t q) -> p s t q", s=SB, t=3),
                                             rowsv[:, u, :, D:ROW].unsqueeze(2).broadcast_to([P, SB, 3, Q]), ALU.mult))
                        link(V.tensor_reduce(e_sc[:, u, :], qq, AX.X, ALU.add))
                        V.tensor_scalar(msg[:, u, :, D], e_sc[:, u, :], 0.0, None, ALU.max)
                        V.tensor_scalar(msg[:, u, :, D + 1], e_sc[:, u, :], -1.0, 0.0, ALU.mult, ALU.max).then_inc(weights_ready, 1)
                        _, at = nc.values_load_multi_w_load_instructions(
                            acc_at[:, bass.ds(k, 1), :].rearrange("p k s -> p (k s)"), engines=(DVE_ENGINE,), min_val=0,
                            max_val=(NB - 1) * MW, skip_runtime_bounds_check_because="the block was clamped to NB - 1")
                        for s in range(SB):
                            dve.wait_ge(product, k * SB + s + 1)
                            a = acc[:, bass.ds(at[s], MW)]
                            dve.wait_ge(added, k * SB + s + 4)
                            V.tensor_tensor(a, a, bank[s % 4][:, 0:MW], ALU.add).then_inc(added, 1)
                    assert here[0] == 2 * UN

        graph.close()

        with ExitStack() as pc:
            xg = sb(pc, "xg", [P, GB, D], F32)
            xng = sb(pc, "xng", [P, GB, D], F32)
            xt_f = sb(pc, "xt_f", [P, KC, TOK], F32)
            xh = sb(pc, "xh", [P, 2, KC, TOK], F32R)
            xl = sb(pc, "xl", [P, 2, KC, TOK], F32R)
            h_f = sb(pc, "h_f", [P, 2, 2, TOK], F32)
            h_hi = sb(pc, "h_hi", [P, 2, 2, KC, TOK], F32R)
            h_lo = sb(pc, "h_lo", [P, 2, 2, KC, TOK], F32R)
            NW = 4
            gate_bc = sb(pc, "gate_bc", [P, NW, TOK], F32)
            gate_t = sb(pc, "gate_t", [NE, 2, TOK], F32)
            y_t = xt_f
            lg = sb(pc, "lg", [P, GB, NE], F32)
            lmax = sb(pc, "lmax", [P, GB], F32)
            lexp = gate = lg
            st3 = sb(pc, "st3", [P, GB, 6], F32)
            mv3 = sb(pc, "mv3", [P, GB, 2], F32)
            var3 = sb(pc, "var3", [P, GB], F32)
            sd3 = sb(pc, "sd3", [P, GB], F32)
            rs3 = sb(pc, "rs3", [P, GB], F32)

            c_in, c_var, c_sd, c_xhat, c_xt, c_xtf = (sem(n) for n in ("c_in", "c_var", "c_sd", "c_xhat", "c_xt", "c_xtf"))
            c_split, c_lg, c_sub, c_exp, c_gate = (sem(n) for n in ("c_split", "c_lg", "c_sub", "c_exp", "c_gate"))
            c_gt, c_gtf, c_gout = (sem(n) for n in ("c_gt", "c_gtf", "c_gout"))
            c_bc = [sem(f"c_bc{n}") for n in range(NW)]
            mm_1, mm_2, mm_3 = sem("mm_1"), sem("mm_2"), sem("mm_3")
            relu_1, relu_2, split_1, split_2 = sem("relu_1"), sem("relu_2"), sem("split_1"), sem("split_2")
            turn, c_y, c_yt, c_fin, c_out, dve_c = sem("turn"), sem("c_y"), sem("c_yt"), sem("c_fin"), sem("c_out"), sem("dve_c")
            accv = acc[:].rearrange("p (b w) -> p b w", w=MW)
            C2 = 2 * NW
            ITC = 7
            GRP = [(2 * ITC + n, GB if 2 * ITC + n < NG - 1 else 1) for n in range(NG - 2 * ITC)]

            def at_block(g, j):
                return bass.ds(g * GB + j, 1)

            def groups(eng, first, body):
                if first is not None:
                    first(0, GB, 0)
                with eng.Fori(0, ITC) as it:
                    body(it * 2, GB, 0, GB)
                    body(it * 2 + 1, GB, 1, GB)
                for n, (g, nb) in enumerate(GRP):
                    body(g, nb, g % 2, GRP[n + 1][1] if n + 1 < len(GRP) else 0)

            block = pc.enter_context(nc.Block())

            @block.sync
            def _(sp):
                def load(g, nb, par):
                    rows_g = bass.ds(g * TOK, nb * P)
                    sp.dma_start(xng[:, 0:nb, :], table_ap[rows_g, 0:D].rearrange("(b p) d -> p b d", p=P)).then_inc(c_in, 16)
                    if nb == GB:
                        sp.dma_start(xg[:], x[rows_g, :].rearrange("(b p) d -> p b d", p=P)).then_inc(c_in, 16)
                    else:
                        sp.dma_start(xg[0:TAIL, 0, :], x[(NB - 1) * P:N, :]).then_inc(c_in, 16)

                def body(g, nb, par, nxt):
                    if nxt:
                        sp.wait_ge(c_xt, g + 1)
                        load(g + 1, nxt, 1 - par)
                    sp.wait_ge(c_gout, 16 * (g + 1))
                    sp.sem_inc(turn, 1)
                    for e in range(NE):
                        sp.wait_ge(split_2, g * 16 + 2 * e + 2)
                        sp.sem_inc(turn, 1)
                        sp.dma_start(gate_bc[:, e % NW, 0:nb * P], gates_ap[e:e + 1, bass.ds(g * TOK, nb * P)].rearrange("a n -> (a n)").partition_broadcast(P)
                                     ).then_inc(c_bc[e % NW], 16)

                groups(sp, load, body)

            @block.gpsimd
            def _(pool):
                def gates_out(g, nb, par):
                    pool.wait_ge(c_gtf, g + 1)
                    pool.dma_start(gates_ap[:, bass.ds(g * TOK, nb * P)], gate_t[:, par, 0:nb * P]).then_inc(c_gout, 16)

                def body(g, nb, par, nxt):
                    if nxt:
                        gates_out(g + 1, nxt, 1 - par)
                    pool.wait_ge(c_fin, g + 3)
                    if nb == GB:
                        pool.dma_start(out[bass.ds(g * TOK, TOK), :].rearrange("(b p) d -> p b d", p=P),
                                       accv[:, bass.ds(g * GB, GB), 0:D]).then_inc(c_out, 16)
                    else:
                        pool.dma_start(out[(NB - 1) * P:N, :], accv[0:TAIL, NB - 1, 0:D]).then_inc(c_out, 16)

                groups(pool, gates_out, body)
                pool.wait_ge(c_out, 16 * NG)
                pool.wait_ge(c_gout, 16 * NG)

            @block.tensor
            def _(pe):
                M = nc.tensor.matmul
                pe.sem_inc(mm_3, 2)
                pe.sem_inc(c_yt, 1)

                def turn(g, nb, par):
                    pe.wait_ge(c_xhat, g + 1)
                    pe.wait_ge(c_fin, g + 1)
                    for k in range(KC):
                        for j in range(nb):
                            mm = nc.tensor.transpose(bank[6 + k][:, j * P:(j + 1) * P], xg[:, j, k * P:(k + 1) * P], ident[:])
                    mm.then_inc(c_xt, 1)

                def logits(g, nb, par):
                    pe.wait_ge(c_xtf, 2 * (g + 1))
                    for j in range(nb):
                        for k in range(KC):
                            mm = M(bank[6][:, j * NE:(j + 1) * NE], xt_f[:, k, j * P:(j + 1) * P], wr_sb[:, k, :],
                                   start=(k == 0), stop=(k == KC - 1))
                    mm.then_inc(c_lg, 1)

                def turn_gates(g, nb, par):
                    pe.wait_ge(c_gate, g + 1)
                    for j in range(nb):
                        mm = nc.tensor.transpose(bank[7][0:NE, j * P:(j + 1) * P], gate[:, j, :], ident[:])
                    mm.then_inc(c_gt, 1)

                def three(out_, n, k, m, hi, lo, first, last):
                    a, b = wh[:, n, k * D + m * P:k * D + (m + 1) * P], wl[:, n, k * D + m * P:k * D + (m + 1) * P]
                    M(out_, a, hi, start=first, stop=False)
                    M(out_, a, lo, start=False, stop=False)
                    return M(out_, b, hi, start=False, stop=last)

                def body(g, nb, par, nxt):
                    T = nb * P

                    def layer_1(e):
                        pe.wait_ge(c_split, g + 1)
                        for m in range(2):
                            pe.wait_ge(relu_1, g * 16 + e * 2 + m + 1)
                            for k in range(KC):
                                mm = three(bank[m][:, 0:T], e, k, m, xh[:, par, k, 0:T], xl[:, par, k, 0:T], k == 0, k == KC - 1)
                            mm.then_inc(mm_1, 1)

                    def layer_2(e):
                        pe.wait_ge(split_1, g * 16 + e * 2 + 2 + 2)
                        for m in range(2):
                            pe.wait_ge(relu_2, g * 16 + e * 2 + m + 1)
                            for k in range(KC):
                                mm = three(bank[2 + m][:, 0:T], NE + e, k, m, h_hi[:, 0, e % 2, k, 0:T], h_lo[:, 0, e % 2, k, 0:T], k == 0, k == KC - 1)
                            mm.then_inc(mm_2, 1)

                    def layer_3(e):
                        if e == 0:
                            pe.wait_ge(c_gtf, g + 1)
                            pe.wait_ge(c_y, 2 * g + 2)
                            for m in range(KC):
                                M(bank[4 + m][:, 0:T], bo_sb[:, m * P:(m + 1) * P], gate_t[:, par, 0:T], start=True, stop=False)
                        pe.wait_ge(split_2, g * 16 + e * 2 + 2 + C2)
                        for m in range(KC):
                            for k in range(KC):
                                mm = three(bank[4 + m][:, 0:T], 2 * NE + e, k, m, h_hi[:, 1, e % 2, k, 0:T], h_lo[:, 1, e % 2, k, 0:T],
                                           False, e == NE - 1 and k == KC - 1)
                        mm.then_inc(mm_3, 1)

                    for e in range(NE + 2):
                        if e < NE:
                            layer_1(e)
                        if 1 <= e <= NE:
                            layer_2(e - 1)
                        if e >= 2:
                            layer_3(e - 2)
                        if nxt and e == 4:
                            turn(g + 1, nxt, 1 - par)
                        if nxt and e == 5:
                            logits(g + 1, nxt, 1 - par)
                        if nxt and e == 7:
                            turn_gates(g + 1, nxt, 1 - par)
                    pe.wait_ge(c_y, 2 * g + 4)
                    if nxt:
                        pe.wait_ge(c_gtf, g + 2)
                    for j in range(nb):
                        for m in range(KC):
                            mm = nc.tensor.transpose(bank[6 + j // 2][:, (j % 2 * KC + m) * P:(j % 2 * KC + m + 1) * P],
                                                     y_t[:, m, j * P:(j + 1) * P], ident[:])
                    mm.then_inc(c_yt, 1)

                def first(g, nb, par):
                    turn(g, nb, par)
                    logits(g, nb, par)
                    turn_gates(g, nb, par)

                groups(pe, first, body)

            @block.scalar
            def _(act):
                A = nc.scalar.activation
                act.sem_inc(relu_1, 2)
                act.sem_inc(relu_2, 2)
                act.sem_inc(c_y, 2)

                def norm(g, nb, par):
                    act.wait_ge(c_var, g + 1)
                    A(sd3[:, 0:nb], var3[:, 0:nb], ACT.Sqrt).then_inc(c_sd, 1)

                def turned(g, nb, par):
                    act.wait_ge(c_xt, g + 1)
                    for k in range(KC):
                        nc.scalar.copy(xt_f[:, k, 0:nb * P], bank[6 + k][:, 0:nb * P]).then_inc(c_xtf, 1)

                def exps(g, nb, par):
                    act.wait_ge(c_sub, g + 1)
                    A(lexp[:, 0:nb, :], lg[:, 0:nb, :], ACT.Exp).then_inc(c_exp, 1)

                def gates(g, nb, par):
                    act.wait_ge(c_gt, g + 1)
                    if not (isinstance(g, int) and g == 0):
                        act.wait_ge(c_gout, 16 * g)
                    nc.scalar.copy(gate_t[:, par, 0:nb * P], bank[7][0:NE, 0:nb * P]).then_inc(c_gtf, 1)

                def body(g, nb, par, nxt):
                    T = nb * P

                    def relu(layer, e, mm, ready, split, more):
                        for m in range(2):
                            n = g * 16 + e * 2 + m + 1
                            act.wait_ge(mm, n)
                            act.wait_ge(split, n + more)
                            A(h_f[:, layer, m, 0:T], bank[2 * layer + m][:, 0:T], ACT.Relu,
                              bias=bn_c[:, layer, 2 * e + m:2 * e + m + 1], scale=bn_s[:, layer, 2 * e + m:2 * e + m + 1]).then_inc(ready, 1)

                    for e in range(NE + 1):
                        if e < NE:
                            relu(0, e, mm_1, relu_1, split_1, 0)
                        if e >= 1:
                            relu(1, e - 1, mm_2, relu_2, split_2, C2 - 2)
                        if nxt and e == 2:
                            norm(g + 1, nxt, 1 - par)
                        if nxt and e == 4:
                            turned(g + 1, nxt, 1 - par)
                        if nxt and e == 6:
                            exps(g + 1, nxt, 1 - par)
                        if nxt and e == 8:
                            gates(g + 1, nxt, 1 - par)
                    act.wait_ge(mm_3, (g + 1) * NE + 2)
                    act.wait_ge(c_yt, g + 1)
                    for m in range(KC):
                        nc.scalar.copy(y_t[:, m, 0:T], bank[4 + m][:, 0:T]).then_inc(c_y, 1)

                
                def first(g, nb, par):
                    norm(g, nb, par)
                    turned(g, nb, par)
                    exps(g, nb, par)
                    gates(g, nb, par)

                groups(act, first, body)

            @block.vector
            def _(dve):
                V = nc.vector
                base = [None, 0, 0]

                def link(ins):
                    base[1] += 1
                    ins.then_inc(dve_c, 1)
                    dve.wait_ge(dve_c, base[0] + base[1])

                dve.sem_inc(split_1, 2)
                dve.sem_inc(split_2, C2)
                dve.sem_inc(c_fin, 2)
                base[0] = 0
                a_sum, r_sum = accv[:, :, D], accv[:, :, D + 1]
                link(V.tensor_tensor(a_sum, a_sum, r_sum, ALU.add))
                link(V.tensor_scalar(a_sum, a_sum, DEN_EPS, None, ALU.add))
                link(V.reciprocal(a_sum, a_sum))
                link(V.tensor_tensor(r_sum, r_sum, a_sum, ALU.mult))

                def residual(g, nb, par, stage):
                    a = [accv[:, at_block(g, j), 0:D].rearrange("p b d -> p (b d)") for j in range(nb)]
                    column = lambda j, c: accv[:, at_block(g, j), c:c + 1].rearrange("p b d -> p (b d)")
                    if stage == 0:
                        dve.wait_ge(c_in, 32 * (g + 1))
                        for j in range(nb):
                            last = V.scalar_tensor_tensor(out=a[j], in0=a[j], scalar=column(j, D), in1=xg[:, j, :], op0=ALU.mult, op1=ALU.add)
                        link(last)
                    if stage == 1:
                        for j in range(nb):
                            last = V.scalar_tensor_tensor(out=a[j], in0=xng[:, j, :], scalar=column(j, D + 1), in1=a[j], op0=ALU.mult, op1=ALU.add)
                        link(last)
                        V.memset(var3[:, 0:1], 0.0)
                    if stage == 2:
                        for j in range(nb):
                            last = V.bn_stats(st3[:, j, :], a[j])
                        link(last)
                        V.memset(var3[:, 0:1], 0.0)
                        for j in range(nb):
                            last = V.bn_aggr(mv3[:, j, :], st3[:, j, :])
                        link(last)
                        V.tensor_scalar(var3[:, 0:nb], mv3[:, 0:nb, 1], LN_EPS, None, ALU.add).then_inc(c_var, 1)

                def norm(g, nb, par):
                    dve.wait_ge(c_sd, g + 1)
                    link(V.reciprocal(rs3[:, 0:nb], sd3[:, 0:nb]))
                    for j in range(nb):
                        last = V.tensor_scalar(xg[:, j, :], accv[:, at_block(g, j), 0:D].rearrange("p b d -> p (b d)"),
                                               mv3[:, j, 0:1], rs3[:, j:j + 1], ALU.subtract, ALU.mult)
                    last.then_inc(c_xhat, 1)

                def split_x(g, nb, par):
                    dve.wait_ge(c_xtf, 2 * (g + 1))
                    T = nb * P
                    link(V.tensor_copy(xh[:, par, :, 0:T], xt_f[:, :, 0:T]))
                    V.tensor_tensor(xl[:, par, :, 0:T], xt_f[:, :, 0:T], xh[:, par, :, 0:T].bitcast(F32), ALU.subtract).then_inc(c_split, 1)

                def softmax_1(g, nb, par):
                    dve.wait_ge(c_lg, g + 1)
                    l = lg[:, 0:nb, :]
                    link(V.tensor_tensor(l, bank[6][:, 0:nb * NE].rearrange("p (b e) -> p b e", e=NE),
                                         br_sb[:].unsqueeze(1).broadcast_to([P, nb, NE]), ALU.add))
                    link(V.tensor_reduce(lmax[:, 0:nb], l, AX.X, ALU.max))
                    V.tensor_tensor(l, l, lmax[:, 0:nb].unsqueeze(2).broadcast_to([P, nb, NE]), ALU.subtract).then_inc(c_sub, 1)

                def softmax_2(g, nb, par):
                    dve.wait_ge(c_exp, g + 1)
                    link(V.tensor_reduce(lmax[:, 0:nb], lexp[:, 0:nb, :], AX.X, ALU.add))
                    link(V.reciprocal(lmax[:, 0:nb], lmax[:, 0:nb]))
                    V.tensor_tensor(gate[:, 0:nb, :], lexp[:, 0:nb, :], lmax[:, 0:nb].unsqueeze(2).broadcast_to([P, nb, NE]), ALU.mult).then_inc(c_gate, 1)

                def body(g, nb, par, nxt):
                    T = nb * P

                    def split_1_(e):
                        for m in range(2):
                            n = g * 16 + e * 2 + m
                            dve.wait_ge(relu_1, n + 3)
                            hi = h_hi[:, 0, e % 2, m, 0:T]
                            link(V.tensor_copy(hi, h_f[:, 0, m, 0:T]))
                            V.tensor_tensor(h_lo[:, 0, e % 2, m, 0:T], h_f[:, 0, m, 0:T], hi.bitcast(F32), ALU.subtract).then_inc(split_1, 1)

                    def split_2_(e):
                        for m in range(2):
                            n = g * 16 + e * 2 + m
                            dve.wait_ge(relu_2, n + 3)
                            if m == 0:
                                dve.wait_ge(c_bc[e % NW], (g * 2 + e // NW + 1) * 16)
                                dve.wait_ge(mm_3, g * NE + e + 1)
                            link(V.tensor_tensor(h_f[:, 1, m, 0:T], h_f[:, 1, m, 0:T], gate_bc[:, e % NW, 0:T], ALU.mult))
                            hi = h_hi[:, 1, e % 2, m, 0:T]
                            link(V.tensor_copy(hi, h_f[:, 1, m, 0:T]))
                            V.tensor_tensor(h_lo[:, 1, e % 2, m, 0:T], h_f[:, 1, m, 0:T], hi.bitcast(F32), ALU.subtract).then_inc(split_2, 1)

                    for e in range(NE + 1):
                        if e < NE:
                            split_1_(e)
                        if e >= 1:
                            split_2_(e - 1)
                        if nxt and e < 3:
                            residual(g + 1, nxt, 1 - par, e)
                        if nxt and e == 3:
                            norm(g + 1, nxt, 1 - par)
                        if nxt and e == 5:
                            split_x(g + 1, nxt, 1 - par)
                        if nxt and e == 6:
                            softmax_1(g + 1, nxt, 1 - par)
                        if nxt and e == 7:
                            softmax_2(g + 1, nxt, 1 - par)
                    dve.wait_ge(c_yt, g + 2)
                    for j in range(nb):
                        a = accv[:, at_block(g, j), 0:D].rearrange("p b d -> p (b d)")
                        last = V.tensor_tensor(a, a, bank[6 + j // 2][:, j % 2 * D:(j % 2 + 1) * D], ALU.add)
                    last.then_inc(c_fin, 1)

                for stage in range(3):
                    residual(0, GB, 0, stage)
                norm(0, GB, 0)
                split_x(0, GB, 0)
                softmax_1(0, GB, 0)
                softmax_2(0, GB, 0)
                ahead = base[1]
                LINKS = 4 + 1 + 1 + 2 + 2 + 2 * NE + 4 * NE
                with dve.Fori(0, ITC) as it:
                    base[0], base[1] = it * (2 * LINKS) + ahead, 0
                    body(it * 2, GB, 0, GB)
                    body(it * 2 + 1, GB, 1, GB)
                    assert base[1] == 2 * LINKS, base[1]
                base[0], base[1] = ahead + ITC * 2 * LINKS, 0
                for n, (g, nb) in enumerate(GRP):
                    body(g, nb, g % 2, GRP[n + 1][1] if n + 1 < len(GRP) else 0)


_BN1 = ["L0_ffn_b1", "L0_ffn_g1", "L0_ffn_be1", "L0_ffn_m1", "L0_ffn_v1"]
_BN2 = ["L0_ffn_b2", "L0_ffn_g2", "L0_ffn_be2", "L0_ffn_m2", "L0_ffn_v2"]
_INS = ["x", "src", "dst", "L0_gnn_W_dis", "L0_ffn_Wr", "L0_ffn_br", *_BN1, *_BN2, "L0_ffn_W1", "L0_ffn_W2", "L0_ffn_Wo", "L0_ffn_bo"]


def kernel(**inputs):
    import numpy as np
    import concourse.bacc as bacc
    from concourse import mybir as mb
    from concourse.bass_utils import run_bass_kernel_spmd

    nc = bacc.Bacc("TRN2", target_bir_lowering=False, num_devices=1)
    arrays, a = {}, {}
    for name in _INS:
        v = np.ascontiguousarray(inputs[name])
        arrays[f"in_{name}"] = v
        a[name] = nc.dram_tensor(f"in_{name}", v.shape, mb.dt.from_np(v.dtype), kind="ExternalInput").ap()
    out = nc.dram_tensor("out", arrays["in_x"].shape, mb.dt.float32, kind="ExternalOutput").ap()
    graph_mixture(nc, a["x"], a["src"], a["dst"], a["L0_gnn_W_dis"], a["L0_ffn_Wr"], a["L0_ffn_br"],
                  [a[n] for n in _BN1], [a[n] for n in _BN2], a["L0_ffn_W1"], a["L0_ffn_W2"], a["L0_ffn_Wo"], a["L0_ffn_bo"], out)
    r = run_bass_kernel_spmd(nc, [arrays], core_ids=[0])
    return r.results[0]["out"]
```

```python
from contextlib import ExitStack

import concourse.bass as bass
from concourse import mybir
from concourse.alu_op_type import AluOpType as ALU

ACT = mybir.ActivationFunctionType
AX = mybir.AxisListType
F32 = mybir.dt.float32
F32R = mybir.dt.float32r
BF16 = mybir.dt.bfloat16
I32 = mybir.dt.int32
DVE_ENGINE = mybir.EngineType.DVE
PE_ENGINE = mybir.EngineType.PE

P = 128


def graph_mixture(nc, x, src, dst, w_dis, wr, br, bn1, bn2, w1, w2, wo, bo, out):
    N, D = x.shape
    E = src.shape[0]
    Q = w_dis.shape[0]
    NE = wr.shape[1]
    KC = D // P
    NB = -(-N // P)
    TAIL = N - (NB - 1) * P
    NT = -(-E // P)
    TC = -(-NT // P)
    FULL = (TC - 1) * P
    LAST = NT - 1 - FULL
    ETAIL = E - (NT - 1) * P
    SB = 8
    UN = 2
    STEPS = -(-(NT + NB - 1) // (SB * UN)) * SB * UN
    NBATCH = STEPS // SB
    SH = STEPS // 2
    ROW = D + Q
    MW = D + 2
    LN_EPS, BN_EPS, DEN_EPS = 1e-5, 1e-3, 0.01
    PAD = float(1 << 20)
    GB = 3
    NG = -(-NB // GB)
    TOK = GB * P
    LC = 8
    CH = (NB - 1) // LC
    assert SH <= 512 and NB - (NG - 1) * GB == 1 and (NB - 1) % (2 * LC) == 0

    xn_table = nc.dram_tensor("xn_table", [NB * P, ROW], F32)
    dst_rows = nc.dram_tensor("dst_rows", [NBATCH, SB * P], BF16)
    gate_rows = nc.dram_tensor("gate_rows", [NE, NB * P + 2 * P], F32)
    table_ap, rows_ap, gates_ap = xn_table.ap(), dst_rows.ap(), gate_rows.ap()

    top, graph = ExitStack(), ExitStack()
    with top:
        def sem(name):
            return top.enter_context(nc.semaphore(name))

        def sb(ctx, name, shape, dt):
            return ctx.enter_context(nc.sbuf_tensor(name, shape, dt, side="right" if ctx is graph else "left"))

        bank = [top.enter_context(nc.psum_tensor(f"bank{i}", [P, 512], F32)) for i in range(8)]

        wh = sb(top, "wh", [P, 3 * NE, KC * D], F32R)
        wl = sb(top, "wl", [P, 3 * NE, KC * D], F32R)
        ident = sb(top, "ident", [P, P], F32)
        bn_s = sb(top, "bn_s", [P, 2, 2 * NE], F32)
        bn_c = sb(top, "bn_c", [P, 2, 2 * NE], F32)
        wr_sb = sb(top, "wr_sb", [P, KC, NE], F32)
        br_sb = sb(top, "br_sb", [P, NE], F32)
        bo_sb = sb(top, "bo_sb", [NE, D], F32)

        top.enter_context(graph)
        src_step = sb(graph, "src_step", [P, NBATCH, SB], I32)
        dst_step = sb(graph, "dst_step", [P, NBATCH, SB], F32)
        q_parts = sb(graph, "q_parts", [P, NB * 3 * Q], BF16)
        at = sb(graph, "at", [P, NBATCH, SB], I32)
        acc_at, q_at = at[0:1], at[32:33]
        many = sb(graph, "many", [P, 1], I32)
        iota = sb(graph, "iota", [P, P], F32)
        lane = sb(graph, "lane", [P, 1], F32)

        with ExitStack() as pa:
            x_tile = sb(pa, "x_tile", [P, 2, LC, D], F32)
            xnq = sb(pa, "xnq", [P, 2, LC, ROW], F32)
            raw2 = sb(pa, "raw2", [P, 2, KC * D], F32)
            late = xnq[:].rearrange("p a b r -> p (a b r)")[:, 2 * LC * ROW - 4 * KC * D:]
            raw = [raw2[:, 0, :], raw2[:, 1, :]] + [late[:, n * KC * D:(n + 1) * KC * D] for n in range(4)]
            assert 4 * KC * D <= LC * ROW
            RB = len(raw)
            iota_s = sb(pa, "iota_s", [P, STEPS], F32)
            ones = sb(pa, "ones", [P, P], F32)
            tri = sb(pa, "tri", [P, P], F32)
            dst_i = sb(pa, "dst_i", [P, TC, P], I32)
            src_i = sb(pa, "src_i", [P, TC, P], I32)
            dst_f = sb(pa, "dst_f", [P, TC, P], F32)
            src_f = sb(pa, "src_f", [P, TC, P], F32)
            blk_i = sb(pa, "blk_i", [P, 2, TC], I32)
            blk_j = sb(pa, "blk_j", [P, 2, TC], I32)
            blk_f = sb(pa, "blk_f", [P, 2, TC], F32)
            npair = sb(pa, "npair", [P, TC], F32)
            pref = sb(pa, "pref", [P, 2, TC], F32)
            scan = sb(pa, "scan", [P, TC], F32)
            zero = sb(pa, "zero", [P, TC], F32)
            t_st = sb(pa, "t_st", [P, TC], F32)
            t_en = sb(pa, "t_en", [P, TC], F32)
            t_fs = sb(pa, "t_fs", [P, TC], F32)
            t_fm = sb(pa, "t_fm", [P, TC], F32)
            below = sb(pa, "below", [P, STEPS], F32)
            sel = sb(pa, "sel", [P, STEPS], F32)
            dclamp = sb(pa, "dclamp", [P, TC * P], F32)
            dpos = dclamp[:].rearrange("p (c e) -> p c e", e=P)
            sels = (sel[:], dclamp[:, 0:STEPS])
            rows_sb = sb(pa, "rows_sb", [P, TC, P], BF16)
            wd_in = sb(pa, "wd_in", [Q, D], F32)
            wd_t = sb(pa, "wd_t", [P, KC, Q], F32)
            par_in = [t[0:2 * NE, n, :].bitcast(F32) for t in (dst_i, src_i) for n in range(5)]
            par = sb(pa, "par", [P, 10, 2 * NE], F32)
            xt = sb(pa, "xt", [P, 2, KC * P], F32)
            stats = sb(pa, "stats", [P, LC, 6], F32)
            mv = sb(pa, "mv", [P, LC, 2], F32)
            var = sb(pa, "var", [P, LC], F32)
            sd = sb(pa, "sd", [P, LC], F32)
            rstd = sb(pa, "rstd", [P, LC], F32)
            qr = sb(pa, "qr", [P, LC * Q], F32)
            qr2 = sb(pa, "qr2", [P, LC * Q], F32)
            bn_v = sb(pa, "bn_v", [P, 2, 2 * NE], F32)
            bn_d = sb(pa, "bn_d", [P, 2, 2 * NE], F32)

            edges_in, small_in, x_in = sem("edges_in"), sem("small_in"), [sem("x_in0"), sem("x_in1")]
            tail_cleared = sem("tail_cleared")
            raw_in = [sem(f"raw_in{n}") for n in range(RB)]
            hi_done, lo_done = sem("hi_done"), sem("lo_done")
            cleared, consts = sem("cleared"), sem("consts")
            dve_a, act_a, pool_a = sem("dve_a"), sem("act_a"), sem("pool_a")
            n_ready, pref_done = sem("n_ready"), sem("pref_done")
            dprime, sel_ready, sel_used = sem("dprime"), sem("sel_ready"), sem("sel_used")
            evac, rowt_done, rowt_copied, rows_out = sem("evac"), sem("rowt_done"), sem("rowt_copied"), sem("rows_out")
            part_done, bn_var, bn_sd = sem("part_done"), sem("bn_var"), sem("bn_sd")
            var_ready, sd_ready, xn_ready = sem("var_ready"), sem("sd_ready"), sem("xn_ready")
            xt_done, xt_copied, q_done, q_copied = sem("xt_done"), sem("xt_copied"), sem("q_done"), sem("q_copied")
            table_out, xnq_free = [sem("table_out0"), sem("table_out1")], sem("xnq_free")

            def chunks(eng, body):
                with eng.Fori(0, CH // 2) as it:
                    body(it * 2, LC, 0)
                    body(it * 2 + 1, LC, 1)
                body(CH, 1, 0)

            block = pa.enter_context(nc.Block())

            @block.sync
            def _(sp):
                sp.wait_ge(cleared, 2)
                for a, t in ((dst, dst_i), (src, src_i)):
                    sp.dma_start(t[:, 0:TC - 1, :], a[0:FULL * P].rearrange("(c p e) -> p c e", p=P, e=P)).then_inc(edges_in, 16)
                    sp.dma_start(t[0:LAST, TC - 1, :], a[FULL * P:(NT - 1) * P].rearrange("(p e) -> p e", e=P)).then_inc(edges_in, 16)
                    sp.dma_start(t[LAST:LAST + 1, TC - 1, 0:ETAIL], a[(NT - 1) * P:E].rearrange("(p e) -> p e", p=1)).then_inc(edges_in, 16)
                sp.dma_start(wd_in[:], w_dis).then_inc(small_in, 16)
                sp.dma_start(wr_sb[:], wr.rearrange("(k p) e -> p k e", p=P)).then_inc(small_in, 16)
                sp.dma_start(br_sb[:], br.partition_broadcast(P)).then_inc(small_in, 16)
                sp.dma_start(bo_sb[:], bo).then_inc(small_in, 16)

                def load_x(c, par):
                    sp.dma_start(x_tile[:, par], x[bass.ds(c * (LC * P), LC * P), :].rearrange("(b p) d -> p b d", p=P)).then_inc(x_in[par], 16)

                def load_w(n):
                    if n >= RB:
                        sp.wait_ge(lo_done, n - RB + 1)
                    sp.dma_start(raw[n % RB].rearrange("p (k h) -> p k h", k=KC),
                                 (w1, w2, wo)[n // NE][n % NE].rearrange("(k p) h -> p k h", p=P)).then_inc(raw_in[n % RB], 16)

                for n in range(RB):
                    load_w(n)
                load_x(0, 0)
                sp.wait_ge(n_ready, 1)
                for n, a in enumerate((*bn1, *bn2)):
                    sp.dma_start(par_in[n], a.rearrange("e (m p) -> (e m) p", p=P)).then_inc(small_in, 16)
                load_x(1, 1)
                for n in range(RB, 3 * NE):
                    load_w(n)
                with sp.Fori(1, CH // 2) as it:
                    for par_ in range(2):
                        sp.wait_ge(xn_ready, it * 2 + par_ - 1)
                        load_x(it * 2 + par_, par_)
                sp.wait_ge(tail_cleared, 1)
                sp.dma_start(x_tile[0:TAIL, 0, 0, :], x[(NB - 1) * P:N, :]).then_inc(x_in[0], 16)
                sp.wait_ge(rowt_copied, TC)
                flat = rows_ap.rearrange("k (s e) -> (k s) e", e=P)
                whole = STEPS // P
                sp.dma_start(flat[0:whole * P, :].rearrange("(c p) e -> p c e", p=P), rows_sb[:, 0:whole, :]).then_inc(rows_out, 16)
                sp.dma_start(flat[whole * P:STEPS, :], rows_sb[0:STEPS - whole * P, whole, :]).then_inc(rows_out, 16)
                sp.wait_ge(rows_out, 32)

            @block.gpsimd
            def _(pool):
                pool.sem_inc(xnq_free, 2)
                nc.gpsimd.memset(dst_i[:, TC - 1, :], -int(PAD)).then_inc(cleared, 1)
                nc.gpsimd.memset(src_i[:, TC - 1, :], 0).then_inc(cleared, 1)
                nc.gpsimd.memset(ones[:], 1.0).then_inc(pool_a, 1)
                nc.gpsimd.memset(zero[:], 0.0).then_inc(pool_a, 1)
                pool.wait_ge(pool_a, 1)
                nc.gpsimd.affine_select(out=ident[:], in_=ones[:], compare_op=ALU.is_equal, fill=0.0, base=0,
                                        pattern=[[-1, P]], channel_multiplier=1).then_inc(consts, 1)
                nc.gpsimd.affine_select(out=tri[:], in_=ones[:], compare_op=ALU.is_gt, fill=0.0, base=0,
                                        pattern=[[1, P]], channel_multiplier=-1).then_inc(consts, 1)
                nc.gpsimd.iota(iota_s[:], pattern=[[1, STEPS]], base=0, channel_multiplier=0,
                               allow_small_or_imprecise_dtypes=True).then_inc(consts, 1)
                nc.gpsimd.iota(iota[:], pattern=[[1, P]], base=0, channel_multiplier=0,
                               allow_small_or_imprecise_dtypes=True).then_inc(consts, 1)
                nc.gpsimd.iota(lane[:], pattern=[[0, 1]], base=0, channel_multiplier=1,
                               allow_small_or_imprecise_dtypes=True).then_inc(consts, 1)
                for n in range(3 * NE):
                    pool.wait_ge(hi_done, n + 1)
                    nc.gpsimd.tensor_tensor(out=wl[:, n, :], in0=raw[n % RB], in1=wh[:, n, :].bitcast(F32),
                                            op=ALU.subtract).then_inc(lo_done, 1)

                def body(c, nb, par_):
                    pool.wait_ge(q_copied, c + 1)
                    pool.dma_start(table_ap[bass.ds(c * (LC * P), nb * P), :].rearrange("(b p) r -> p b r", p=P),
                                   xnq[:, par_, 0:nb, :]).then_inc(table_out[par_], 16)
                    pool.wait_ge(table_out[par_], (c - par_) * 8 + 16)
                    pool.sem_inc(xnq_free, 1)

                chunks(pool, body)

            @block.scalar
            def _(act):
                for n in range(3 * NE):
                    act.wait_ge(raw_in[n % RB], 16 * (n // RB + 1))
                    nc.scalar.copy(wh[:, n, :], raw[n % RB]).then_inc(hi_done, 1)

                def deviations(c):
                    act.wait_ge(var_ready, c + 1)
                    nc.scalar.activation(sd[:], var[:], ACT.Sqrt).then_inc(sd_ready, 1)

                def body(c, nb, par_):
                    for j in range(nb):
                        act.wait_ge(xt_done, c * LC + j + 1)
                        nc.scalar.copy(xt[:, j % 2, :], bank[j % 2][:, 0:KC * P]).then_inc(xt_copied, 1)
                        if j == LC - 4:
                            deviations(c + 1)
                    act.wait_ge(q_done, c * LC + nb)
                    nc.scalar.mul(xnq[:, par_, 0:nb, D:ROW], bank[2][:, 0:nb * Q].rearrange("p (b q) -> p b q", q=Q), 0.25).then_inc(q_copied, 1)

                deviations(0)
                act.wait_ge(bn_var, 1)
                nc.scalar.activation(bn_d[:], bn_v[:], ACT.Sqrt).then_inc(bn_sd, 1)
                chunks(act, body)

            @block.tensor
            def _(pe):
                pe.wait_ge(consts, 2)
                pe.wait_ge(n_ready, 1)
                nc.tensor.matmul(bank[6][:, 0:TC], tri[:], npair[:], start=True, stop=True)
                nc.tensor.matmul(bank[6][:, TC:2 * TC], ones[:], npair[:], start=True, stop=True).then_inc(pref_done, 1)
                pe.wait_ge(dprime, 1)
                for c in range(TC):
                    pe.wait_ge(sel_ready, c + 1)
                    for n, lhs in enumerate((src_f[:, c, :], dst_f[:, c, :], t_fs[:, c:c + 1].broadcast_to([P, P]))):
                        for h in range(2):
                            mm = nc.tensor.matmul(bank[2 * n + h][:, 0:SH], lhs, sels[c % 2][:, h * SH:(h + 1) * SH],
                                                  start=(c == 0), stop=(c == TC - 1))
                    mm.then_inc(sel_used, 1)
                pe.wait_ge(small_in, 16 * 14)
                for n in range(10):
                    nc.tensor.transpose(bank[7][:, n * 2 * NE:(n + 1) * 2 * NE], par_in[n], ident[0:2 * NE, 0:2 * NE])
                for k in range(KC):
                    mm = nc.tensor.transpose(bank[7][:, 160 + k * Q:160 + (k + 1) * Q], wd_in[:, k * P:(k + 1) * P], ident[0:Q, 0:Q])
                mm.then_inc(part_done, 1)
                pe.wait_ge(evac, 1)
                for c in range(TC):
                    if c >= 2:
                        pe.wait_ge(rowt_copied, c - 1)
                    else:
                        pe.wait_ge(bn_var, 1)
                    nc.tensor.transpose(bank[6 + c % 2][:, 0:P], dclamp[:, c * P:(c + 1) * P], ident[:]).then_inc(rowt_done, 1)
                def body(c, nb, par_):
                    pe.wait_ge(xn_ready, c + 1)
                    for j in range(nb + 1):
                        if j < nb:
                            if j >= 2:
                                pe.wait_ge(xt_copied, c * LC + j - 1)
                            for k in range(KC):
                                mm = nc.tensor.transpose(bank[j % 2][:, k * P:(k + 1) * P], xnq[:, par_, j, k * P:(k + 1) * P], ident[:])
                            mm.then_inc(xt_done, 1)
                        if j >= 1:
                            pe.wait_ge(xt_copied, c * LC + j)
                            for k in range(KC):
                                mm = nc.tensor.matmul(bank[2][:, (j - 1) * Q:j * Q], xt[:, (j - 1) % 2, k * P:(k + 1) * P], wd_t[:, k, :],
                                                      start=(k == 0), stop=(k == KC - 1))
                            mm.then_inc(q_done, 1)

                chunks(pe, body)

            @block.vector
            def _(dve):
                done = [0]

                def link(ins):
                    done[0] += 1
                    ins.then_inc(dve_a, 1)
                    dve.wait_ge(dve_a, done[0])

                V = nc.vector
                dve.wait_ge(edges_in, 96)
                V.tensor_copy(dst_f[:], dst_i[:])
                link(V.tensor_copy(src_f[:], src_i[:]))
                link(V.tensor_scalar(dpos, dst_f[:], 0.0, 2 * PAD, ALU.is_lt, ALU.mult))
                link(V.tensor_tensor(dpos, dpos, dst_f[:], ALU.add))
                V.tensor_reduce(blk_i[:, 0, :], dpos, AX.X, ALU.min)
                link(V.tensor_reduce(blk_i[:, 1, :], dst_f[:], AX.X, ALU.max))
                link(V.tensor_scalar(blk_j[:], blk_i[:], 7, None, ALU.arith_shift_right))
                link(V.tensor_copy(blk_f[:], blk_j[:]))
                link(V.tensor_scalar(blk_f[:, 1, :], blk_f[:, 1, :], -1.0, 1.0, ALU.max, ALU.add))
                link(V.tensor_tensor(npair[:], blk_f[:, 1, :], blk_f[:, 0, :], ALU.subtract))
                V.tensor_scalar(npair[:], npair[:], 0.0, None, ALU.max).then_inc(n_ready, 1)
                dve.wait_ge(pref_done, 1)
                dve.wait_ge(pool_a, 2)
                link(V.tensor_copy(pref[:].rearrange("p a c -> p (a c)"), bank[6][:, 0:2 * TC]))
                link(V.tensor_tensor_scan(scan[:], pref[:, 1, :], zero[:], 0.0, ALU.add, ALU.add))
                link(V.tensor_scalar(many[:], scan[:, TC - 1:TC], float(STEPS), None, ALU.is_gt))
                link(V.tensor_tensor(scan[:], scan[:], pref[:, 1, :], ALU.subtract))
                link(V.tensor_tensor(t_st[:], scan[:], pref[:, 0, :], ALU.add))
                V.tensor_tensor(t_en[:], t_st[:], npair[:], ALU.add)
                link(V.tensor_tensor(t_fs[:], blk_f[:, 0, :], t_st[:], ALU.subtract))
                link(V.tensor_scalar(t_fm[:], t_fs[:], -float(P), None, ALU.mult))
                for c in range(TC):
                    last = V.tensor_scalar(dst_f[:, c, :], dst_f[:, c, :], t_fm[:, c:c + 1], None, ALU.add)
                last.then_inc(dprime, 1)
                dve.wait_ge(consts, 5)
                for c in range(TC):
                    if c >= 1:
                        dve.wait_ge(sel_ready, c)
                    link(V.tensor_scalar(below[:], iota_s[:], t_en[:, c:c + 1], None, ALU.is_lt))
                    if c >= 2:
                        dve.wait_ge(sel_used, c - 1)
                    V.scalar_tensor_tensor(out=sels[c % 2], in0=iota_s[:], scalar=t_st[:, c:c + 1], in1=below[:],
                                           op0=ALU.is_ge, op1=ALU.mult).then_inc(sel_ready, 1)
                per = 8
                base = done[0]
                here = [0, 0]

                def link_c(ins):
                    here[1] += 1
                    ins.then_inc(dve_a, 1)
                    dve.wait_ge(dve_a, here[0] + here[1])

                def norm(c, nb, par_):
                    dve.wait_ge(x_in[par_], (c - par_) * 8 + 16)
                    for j in range(nb):
                        last = V.bn_stats(stats[:, j, :], x_tile[:, par_, j, :])
                    link_c(last)
                    V.memset(scan[:, 0:1], 0.0)
                    for j in range(nb):
                        last = V.bn_aggr(mv[:, j, :], stats[:, j, :])
                    link_c(last)
                    V.tensor_scalar(var[:, 0:nb], mv[:, 0:nb, 1], LN_EPS, None, ALU.add).then_inc(var_ready, 1)
                    dve.wait_ge(sd_ready, c + 1)
                    link_c(V.reciprocal(rstd[:, 0:nb], sd[:, 0:nb]))
                    dve.wait_ge(xnq_free, c + 1)
                    for j in range(nb):
                        last = V.tensor_scalar(xnq[:, par_, j, 0:D], x_tile[:, par_, j, :], mv[:, j, 0:1], rstd[:, j:j + 1], ALU.subtract, ALU.mult)
                    last.then_inc(xn_ready, 1)

                def split_q(c, nb, par_):
                    dve.wait_ge(q_copied, c + 1)
                    qv = xnq[:, par_, 0:nb, D:ROW]
                    qp = q_parts[:, bass.ds(c * (LC * 3 * Q), nb * 3 * Q)].rearrange("p (b t q) -> p b t q", t=3, q=Q)
                    q1 = qr[:, 0:nb * Q].rearrange("p (b q) -> p b q", q=Q)
                    q2 = qr2[:, 0:nb * Q].rearrange("p (b q) -> p b q", q=Q)
                    link_c(V.tensor_copy(qp[:, :, 0, :], qv))
                    link_c(V.tensor_tensor(q1, qv, qp[:, :, 0, :], ALU.subtract))
                    link_c(V.tensor_copy(qp[:, :, 1, :], q1))
                    link_c(V.tensor_tensor(q2, q1, qp[:, :, 1, :], ALU.subtract))
                    link_c(V.tensor_copy(qp[:, :, 2, :], q2))
                    if nb == 1:
                        return
                    assert here[1] % per == 0, here

                here[0] = base
                norm(0, LC, 0)
                base += here[1]
                done[0] = base
                dve.wait_ge(sel_used, TC)
                srcv, dstv = (t[:].rearrange("p k s -> p (k s)") for t in (src_step, dst_step))
                atall = at[:].rearrange("p k s -> p (k s)")
                for h in range(2):
                    cols = slice(h * SH, (h + 1) * SH)
                    V.tensor_copy(srcv[:, cols], bank[0 + h][:, 0:SH])
                    V.scalar_tensor_tensor(out=dstv[:, cols], in0=iota_s[:, cols], scalar=-float(P), in1=bank[2 + h][:, 0:SH],
                                           op0=ALU.mult, op1=ALU.add)
                    link(V.tensor_tensor(below[:, cols], iota_s[:, cols], bank[4 + h][:, 0:SH], ALU.add))
                V.tensor_scalar(atall[0:1, :], below[0:1, :], float(NB - 1), float(MW), ALU.min, ALU.mult)
                V.tensor_scalar(atall[32:33, :], below[32:33, :], float(NB - 1), float(3 * Q), ALU.min, ALU.mult)
                V.memset(dclamp[:, STEPS:], -1.0)
                V.tensor_scalar(dclamp[:, 0:STEPS], dstv, -1.0, float(P), ALU.max, ALU.min).then_inc(evac, 1)
                dve.wait_ge(part_done, 1)
                V.tensor_copy(par[:].rearrange("p a b -> p (a b)"), bank[7][:, 0:160])
                link(V.tensor_copy(wd_t[:].rearrange("p k q -> p (k q)"), bank[7][:, 160:160 + KC * Q]))
                pv = par[:].rearrange("p (l n) m -> p l n m", l=2)
                V.tensor_scalar(bn_v[:], pv[:, :, 4, :], BN_EPS, None, ALU.add).then_inc(bn_var, 1)
                for c in range(TC):
                    dve.wait_ge(rowt_done, c + 1)
                    V.tensor_copy(rows_sb[:, c, :], bank[6 + c % 2][:, 0:P]).then_inc(rowt_copied, 1)
                base = done[0]
                dve.wait_ge(lo_done, 3 * NE)
                with dve.Fori(0, CH // 2 - 1) as it:
                    here[0], here[1] = it * (2 * per) + base, 0
                    norm(it * 2 + 1, LC, 1)
                    split_q(it * 2, LC, 0)
                    norm(it * 2 + 2, LC, 0)
                    split_q(it * 2 + 1, LC, 1)
                base += 2 * per * (CH // 2 - 1)
                here[0], here[1] = base, 0
                V.memset(x_tile[:, 0, 0, :], 0.0).then_inc(tail_cleared, 1)
                norm(CH - 1, LC, 1)
                split_q(CH - 2, LC, 0)
                norm(CH, 1, 0)
                split_q(CH - 1, LC, 1)
                split_q(CH, 1, 0)
                base += here[1]
                dve.wait_ge(bn_sd, 1)
                link2 = [0]

                def link_e(ins):
                    link2[0] += 1
                    ins.then_inc(dve_a, 1)
                    dve.wait_ge(dve_a, base + link2[0])

                link_e(V.reciprocal(bn_v[:], bn_d[:]))
                link_e(V.tensor_tensor(bn_s[:], pv[:, :, 1, :], bn_v[:], ALU.mult))
                link_e(V.tensor_tensor(bn_c[:], pv[:, :, 0, :], pv[:, :, 3, :], ALU.subtract))
                link_e(V.tensor_tensor(bn_c[:], bn_c[:], bn_s[:], ALU.mult))
                V.tensor_tensor(bn_c[:], bn_c[:], pv[:, :, 2, :], ALU.add)


        acc = sb(top, "acc", [P, NB * MW], F32)

        with ExitStack() as pb:
            rows = sb(pb, "rows", [P, UN * SB * ROW], F32)
            index = sb(pb, "index", [P, UN, SB], I32)
            hot_t = sb(pb, "hot_t", [P, UN, SB * P], BF16)
            hot = sb(pb, "hot", [P, UN, SB, P], F32)
            e_sc = sb(pb, "e_sc", [P, UN, SB], F32)
            msg = sb(pb, "msg", [P, UN, SB, MW], F32)
            rowsv = rows[:].rearrange("p (u s r) -> p u s r", u=UN, s=SB)

            index_ready, gathered = sem("index_ready"), [sem(f"gathered{u}") for u in range(UN)]
            index_used, bc_in = sem("index_used"), [sem(f"bc_in{u}") for u in range(UN)]
            hot_t_ready, qd_done, weights_ready = sem("hot_t_ready"), sem("qd_done"), sem("weights_ready")
            hot_ready, msg_ready, product, added = sem("hot_ready"), sem("msg_ready"), sem("product"), sem("added")
            gather_turn, cleared_b, dve_b, scaled = sem("gather_turn"), sem("cleared_b"), sem("dve_b"), sem("scaled")
            ITERS = NBATCH // UN

            def batches(eng, body):
                with eng.Fori(0, ITERS - 1) as it:
                    k0, n0 = eng.snap(it * UN), eng.snap(it * (UN * SB))
                    for u in range(UN):
                        body(k0 + u, n0 + u * SB, u, UN)
                for u in range(UN):
                    k = (ITERS - 1) * UN + u
                    body(k, k * SB, u, UN - 1 - u)

            block = pb.enter_context(nc.Block())

            @block.sync
            def _(sp):
                with sp.Fori(0, ITERS) as it:
                    for u in range(UN):
                        k = it * UN + u
                        sp.wait_ge(qd_done, k + 1)
                        sp.dma_start(hot_t[:, u, :], rows_ap[bass.ds(k, 1), :].rearrange("a e -> (a e)").partition_broadcast(P)
                                     ).then_inc(bc_in[u], 16)

            @block.gpsimd
            def _(pool):
                with pool.Fori(0, ITERS) as it:
                    for u in range(UN):
                        k = it * UN + u
                        pool.wait_ge(scaled, k + 1)
                        nc.gpsimd.tensor_copy(index[:, u, :], src_step[:, bass.ds(k, 1), :].rearrange("p k s -> p (k s)")).then_inc(index_ready, 1)
                        pool.wait_ge(index_ready, k + 1)
                        pool.sem_inc(gather_turn, 1)
                        for s in range(SB):
                            pool.indirect_dma_start(out=rowsv[:, u, s, :], out_offset=None, in_=table_ap,
                                                    in_offset=bass.IndirectOffsetOnAxis(ap=index[:, u, s:s + 1], axis=0)).then_inc(gathered[u], 16)

            @block.tensor
            def _(pe):
                def q_of_destinations(k, u):
                    pe.wait_ge(hot_t_ready, k + 1)
                    pe.wait_ge(weights_ready, k + 1)
                    _, at = nc.values_load_multi_w_load_instructions(
                        q_at[:, bass.ds(k, 1), :].rearrange("p k s -> p (k s)"), engines=(PE_ENGINE,), min_val=0,
                        max_val=(NB - 1) * 3 * Q, skip_runtime_bounds_check_because="the block was clamped to NB - 1")
                    for s in range(SB):
                        mm = nc.tensor.matmul(bank[6 + u][:, s * 3 * Q:(s + 1) * 3 * Q], hot_t[:, u, s * P:(s + 1) * P],
                                              q_parts[:, bass.ds(at[s], 3 * Q)], start=True, stop=True)
                    mm.then_inc(qd_done, 1)

                def body(k, n, u, after):
                    pe.wait_ge(hot_ready, k + 1)
                    for s in range(SB):
                        if s == 4 and after >= 2:
                            q_of_destinations(k + 2, u)
                        pe.wait_ge(msg_ready, n + (s + 1))
                        pe.wait_ge(added, n + (s + 1))
                        nc.tensor.matmul(bank[s % 4][:, 0:MW], hot[:, u, s, :], msg[:, u, s, :],
                                         start=True, stop=True).then_inc(product, 1)

                pe.sem_inc(qd_done, UN)
                q_of_destinations(0, 0)
                q_of_destinations(1, 1)
                batches(pe, body)

            @block.scalar
            def _(act):
                act.sem_inc(scaled, UN)
                nc.scalar.activation(acc[:].rearrange("p (b m) -> p b m", m=MW), iota[:, 0:1].unsqueeze(2).broadcast_to([P, NB, MW]),
                                     ACT.Copy, scale=0.0).then_inc(cleared_b, 1)
                with act.Fori(0, ITERS) as it:
                    for u in range(UN):
                        k = it * UN + u
                        act.wait_ge(weights_ready, k + 1 + UN)
                        act.wait_ge(gathered[u], (it + 1) * (16 * SB))
                        for s in range(SB):
                            last = nc.scalar.activation(msg[:, u, s, 0:D], rowsv[:, u, s, 0:D], ACT.Copy,
                                                        scale=msg[:, u, s, D:D + 1]).then_inc(msg_ready, 1)
                        act.wait_ge(msg_ready, k * SB + SB)
                        act.sem_inc(scaled, 1)

            @block.vector
            def _(dve):
                V = nc.vector
                dve.sem_inc(weights_ready, UN)
                dve.sem_inc(added, 4)

                def one_hot_t(k, u):
                    dve.wait_ge(bc_in[u], (k - u) * (16 // UN) + 16)
                    V.tensor_scalar(hot_t[:, u, :], hot_t[:, u, :], lane[:], None, ALU.is_equal).then_inc(hot_t_ready, 1)

                def front(k, u):
                    here = [0]

                    def link(ins):
                        here[0] += 1
                        ins.then_inc(dve_b, 1)
                        dve.wait_ge(dve_b, k * 2 + here[0])

                    dve.wait_ge(qd_done, k + 1 + UN)
                    dve.wait_ge(gathered[u], (k - u) * (16 * SB // UN) + 16 * SB)
                    qq = msg[:, u, :, 0:3 * Q]
                    link(V.tensor_tensor(qq.rearrange("p s (t q) -> p s t q", t=3),
                                         bank[6 + u][:, 0:SB * 3 * Q].rearrange("p (s t q) -> p s t q", s=SB, t=3),
                                         rowsv[:, u, :, D:ROW].unsqueeze(2).broadcast_to([P, SB, 3, Q]), ALU.mult))
                    link(V.tensor_reduce(e_sc[:, u, :], qq, AX.X, ALU.add))
                    V.tensor_scalar(msg[:, u, :, D], e_sc[:, u, :], 0.0, None, ALU.max)
                    V.tensor_scalar(msg[:, u, :, D + 1], e_sc[:, u, :], -1.0, 0.0, ALU.mult, ALU.max).then_inc(weights_ready, 1)

                def one_hot(k, u):
                    V.tensor_tensor(hot[:, u], iota[:].unsqueeze(1).broadcast_to([P, SB, P]),
                                    dst_step[:, bass.ds(k, 1), :].rearrange("p k s -> p (k s)").unsqueeze(2).broadcast_to([P, SB, P]),
                                    ALU.is_equal).then_inc(hot_ready, 1)

                def body(k, n, u, after):
                    if after >= 1:
                        front(k + 1, 1 - u)
                        if after >= 2:
                            one_hot_t(k + 2, u)
                        one_hot(k + 1, 1 - u)
                    _, at = nc.values_load_multi_w_load_instructions(
                        acc_at[:, bass.ds(k, 1), :].rearrange("p k s -> p (k s)"), engines=(DVE_ENGINE,), min_val=0,
                        max_val=(NB - 1) * MW, skip_runtime_bounds_check_because="the block was clamped to NB - 1")
                    for s in range(SB):
                        dve.wait_ge(product, n + (s + 1))
                        a = acc[:, bass.ds(at[s], MW)]
                        dve.wait_ge(added, n + (s + 4))
                        V.tensor_tensor(a, a, bank[s % 4][:, 0:MW], ALU.add).then_inc(added, 1)

                one_hot_t(0, 0)
                front(0, 0)
                one_hot_t(1, 1)
                one_hot(0, 0)
                dve.wait_ge(cleared_b, 1)
                batches(dve, body)

        with ExitStack() as pg:
            BG = 7
            assert NB % BG == 0
            src_c = sb(pg, "src_c", [P, 1], I32)
            dst_c = sb(pg, "dst_c", [P, 1], I32)
            dst_l = sb(pg, "dst_l", [P, 1], F32)
            rows_s = sb(pg, "rows_s", [P, ROW], F32)
            rows_d = sb(pg, "rows_d", [P, ROW], F32)
            msg_g = sb(pg, "msg_g", [P, MW], F32)
            prod_g = sb(pg, "prod_g", [P, Q], F32)
            e_g = sb(pg, "e_g", [P, 1], F32)
            hot_g = sb(pg, "hot_g", [P, BG, P], F32)
            g_idx, g_rows, g_used = sem("g_idx"), sem("g_rows"), sem("g_used")
            g_turn, g_dve, g_hot, g_mm = sem("g_turn"), sem("g_dve"), sem("g_hot"), sem("g_mm")
            NGB = NB // BG
            LG = 3 + 2 * NGB

            def tiles(eng, body, before=None):
                value = eng.value_load(many[0:1, 0:1], min_val=0, max_val=1)
                with eng.If(value > 0):
                    if before:
                        before()
                    with eng.Fori(0, NT - 1) as t:
                        body(t, P)
                    body(NT - 1, ETAIL)

            block = pg.enter_context(nc.Block())

            @block.gpsimd
            def _(pool):
                def body(t, ne):
                    pool.wait_ge(g_used, t + 1)
                    pool.sem_inc(g_turn, 1)
                    for a, c in ((src, src_c), (dst, dst_c)):
                        pool.dma_start(c[0:ne, :], a[bass.ds(t * P, ne)].rearrange("(p e) -> p e", e=1)).then_inc(g_idx, 16)
                    pool.wait_ge(g_idx, 32 * t + 32)
                    pool.sem_inc(g_turn, 1)
                    for c, rows_ in ((src_c, rows_s), (dst_c, rows_d)):
                        pool.indirect_dma_start(out=rows_[0:ne, :], out_offset=None, in_=table_ap,
                                                in_offset=bass.IndirectOffsetOnAxis(ap=c[0:ne, :], axis=0)).then_inc(g_rows, 16)

                tiles(pool, body)

            @block.tensor
            def _(pe):
                def body(t, ne):
                    for c in range(NGB):
                        pe.wait_ge(g_hot, t * NGB + c + 1)
                        for j in range(BG):
                            mm = nc.tensor.matmul(bank[j][:, 0:MW], hot_g[0:ne, j, :], msg_g[0:ne, :], start=True, stop=True)
                        mm.then_inc(g_mm, 1)

                tiles(pe, body)

            @block.vector
            def _(dve):
                V = nc.vector
                dve.sem_inc(g_used, 1)

                def body(t, ne):
                    n = [0]

                    def link(ins):
                        n[0] += 1
                        ins.then_inc(g_dve, 1)
                        dve.wait_ge(g_dve, t * LG + n[0] + 1)

                    dve.wait_ge(g_rows, 32 * t + 32)
                    V.tensor_copy(dst_l[0:ne, :], dst_c[0:ne, :])
                    link(V.tensor_tensor(prod_g[0:ne, :], rows_s[0:ne, D:ROW], rows_d[0:ne, D:ROW], ALU.mult))
                    link(V.tensor_reduce(e_g[0:ne, :], prod_g[0:ne, :], AX.X, ALU.add))
                    V.tensor_scalar(msg_g[0:ne, D:D + 1], e_g[0:ne, :], 0.0, None, ALU.max)
                    link(V.tensor_scalar(msg_g[0:ne, D + 1:MW], e_g[0:ne, :], -1.0, 0.0, ALU.mult, ALU.max))
                    link(V.tensor_scalar(msg_g[0:ne, 0:D], rows_s[0:ne, 0:D], msg_g[0:ne, D:D + 1], None, ALU.mult))
                    for c in range(NGB):
                        for j in range(BG):
                            last = V.tensor_scalar(hot_g[0:ne, j, :], iota[0:ne, :], float(j * P), dst_l[0:ne, :], ALU.add, ALU.is_equal)
                        last.then_inc(g_hot, 1)
                        dve.wait_ge(g_mm, t * NGB + c + 1)
                        if c < NGB - 1:
                            link(V.tensor_scalar(dst_l[0:ne, :], dst_l[0:ne, :], -float(BG * P), None, ALU.add))
                        for j in range(BG):
                            a = acc[:, (c * BG + j) * MW:(c * BG + j + 1) * MW]
                            last = V.tensor_tensor(a, a, bank[j][:, 0:MW], ALU.add)
                        link(last)
                    V.memset(e_g[:], 0.0).then_inc(g_used, 1)
                    assert n[0] == LG, (n[0], LG)

                def clear():
                    V.memset(acc[:], 0.0).then_inc(g_dve, 1)
                    dve.wait_ge(g_dve, 1)

                tiles(dve, body, clear)

        graph.close()

        with ExitStack() as pc:
            xg = sb(pc, "xg", [P, GB, D], F32)
            xng = sb(pc, "xng", [P, GB, D], F32)
            xt_f = sb(pc, "xt_f", [P, KC, TOK], F32)
            xh = sb(pc, "xh", [P, 2, KC, TOK], F32R)
            xl = sb(pc, "xl", [P, 2, KC, TOK], F32R)
            h_f = sb(pc, "h_f", [P, 2, 2, TOK], F32)
            h_hi = sb(pc, "h_hi", [P, 2, 2, KC, TOK], F32R)
            h_lo = sb(pc, "h_lo", [P, 2, 2, KC, TOK], F32R)
            NW = 4
            gate_bc = sb(pc, "gate_bc", [P, NW, TOK], F32)
            gate_t = sb(pc, "gate_t", [NE, 2, TOK], F32)
            y_t = xt_f
            lg = sb(pc, "lg", [P, GB, NE], F32)
            lmax = sb(pc, "lmax", [P, GB], F32)
            lexp = gate = lg
            st3 = sb(pc, "st3", [P, GB, 6], F32)
            mv3 = sb(pc, "mv3", [P, GB, 2], F32)
            var3 = sb(pc, "var3", [P, GB], F32)
            sd3 = sb(pc, "sd3", [P, GB], F32)
            rs3 = sb(pc, "rs3", [P, GB], F32)

            c_in, c_var, c_sd, c_xhat, c_xt, c_xtf = (sem(n) for n in ("c_in", "c_var", "c_sd", "c_xhat", "c_xt", "c_xtf"))
            c_split, c_lg, c_sub, c_exp, c_gate = (sem(n) for n in ("c_split", "c_lg", "c_sub", "c_exp", "c_gate"))
            c_gt, c_gtf, c_gout = (sem(n) for n in ("c_gt", "c_gtf", "c_gout"))
            c_bc = [sem(f"c_bc{n}") for n in range(NW)]
            mm_1, mm_2, mm_3 = sem("mm_1"), sem("mm_2"), sem("mm_3")
            relu_1, relu_2, split_1, split_2 = sem("relu_1"), sem("relu_2"), sem("split_1"), sem("split_2")
            turn, c_y, c_yt, c_fin, c_out, dve_c = sem("turn"), sem("c_y"), sem("c_yt"), sem("c_fin"), sem("c_out"), sem("dve_c")
            accv = acc[:].rearrange("p (b w) -> p b w", w=MW)
            C2 = 2 * NW
            ITC = 7
            GRP = [(2 * ITC + n, GB if 2 * ITC + n < NG - 1 else 1) for n in range(NG - 2 * ITC)]

            def at_block(g, j):
                return bass.ds(g * GB + j, 1)

            def groups(eng, first, body):
                if first is not None:
                    first(0, GB, 0)
                with eng.Fori(0, ITC) as it:
                    body(it * 2, GB, 0, GB)
                    body(it * 2 + 1, GB, 1, GB)
                for n, (g, nb) in enumerate(GRP):
                    body(g, nb, g % 2, GRP[n + 1][1] if n + 1 < len(GRP) else 0)

            block = pc.enter_context(nc.Block())

            @block.sync
            def _(sp):
                def load(g, nb, par):
                    rows_g = bass.ds(g * TOK, nb * P)
                    sp.dma_start(xng[:, 0:nb, :], table_ap[rows_g, 0:D].rearrange("(b p) d -> p b d", p=P)).then_inc(c_in, 16)
                    if nb == GB:
                        sp.dma_start(xg[:], x[rows_g, :].rearrange("(b p) d -> p b d", p=P)).then_inc(c_in, 16)
                    else:
                        sp.dma_start(xg[0:TAIL, 0, :], x[(NB - 1) * P:N, :]).then_inc(c_in, 16)

                def body(g, nb, par, nxt):
                    if nxt:
                        sp.wait_ge(c_xt, g + 1)
                        load(g + 1, nxt, 1 - par)
                    sp.wait_ge(c_gout, 16 * (g + 1))
                    sp.sem_inc(turn, 1)
                    for e in range(NE):
                        sp.wait_ge(split_2, g * 16 + 2 * e + 2)
                        sp.sem_inc(turn, 1)
                        sp.dma_start(gate_bc[:, e % NW, 0:nb * P], gates_ap[e:e + 1, bass.ds(g * TOK, nb * P)].rearrange("a n -> (a n)").partition_broadcast(P)
                                     ).then_inc(c_bc[e % NW], 16)

                groups(sp, load, body)

            @block.gpsimd
            def _(pool):
                def gates_out(g, nb, par):
                    pool.wait_ge(c_gtf, g + 1)
                    pool.dma_start(gates_ap[:, bass.ds(g * TOK, nb * P)], gate_t[:, par, 0:nb * P]).then_inc(c_gout, 16)

                def body(g, nb, par, nxt):
                    if nxt:
                        gates_out(g + 1, nxt, 1 - par)
                    pool.wait_ge(c_fin, g + 3)
                    if nb == GB:
                        pool.dma_start(out[bass.ds(g * TOK, TOK), :].rearrange("(b p) d -> p b d", p=P),
                                       accv[:, bass.ds(g * GB, GB), 0:D]).then_inc(c_out, 16)
                    else:
                        pool.dma_start(out[(NB - 1) * P:N, :], accv[0:TAIL, NB - 1, 0:D]).then_inc(c_out, 16)

                groups(pool, gates_out, body)
                pool.wait_ge(c_out, 16 * NG)
                pool.wait_ge(c_gout, 16 * NG)

            @block.tensor
            def _(pe):
                M = nc.tensor.matmul
                pe.sem_inc(mm_3, 2)
                pe.sem_inc(c_yt, 1)

                def turn(g, nb, par):
                    pe.wait_ge(c_xhat, g + 1)
                    pe.wait_ge(c_fin, g + 1)
                    for k in range(KC):
                        for j in range(nb):
                            mm = nc.tensor.transpose(bank[6 + k][:, j * P:(j + 1) * P], xg[:, j, k * P:(k + 1) * P], ident[:])
                    mm.then_inc(c_xt, 1)

                def logits(g, nb, par):
                    pe.wait_ge(c_xtf, 2 * (g + 1))
                    for j in range(nb):
                        for k in range(KC):
                            mm = M(bank[6][:, j * NE:(j + 1) * NE], xt_f[:, k, j * P:(j + 1) * P], wr_sb[:, k, :],
                                   start=(k == 0), stop=(k == KC - 1))
                    mm.then_inc(c_lg, 1)

                def turn_gates(g, nb, par):
                    pe.wait_ge(c_gate, g + 1)
                    for j in range(nb):
                        mm = nc.tensor.transpose(bank[7][0:NE, j * P:(j + 1) * P], gate[:, j, :], ident[:])
                    mm.then_inc(c_gt, 1)

                def three(out_, n, k, m, hi, lo, first, last):
                    a, b = wh[:, n, k * D + m * P:k * D + (m + 1) * P], wl[:, n, k * D + m * P:k * D + (m + 1) * P]
                    M(out_, a, hi, start=first, stop=False)
                    M(out_, a, lo, start=False, stop=False)
                    return M(out_, b, hi, start=False, stop=last)

                def body(g, nb, par, nxt):
                    T = nb * P

                    def layer_1(e):
                        pe.wait_ge(c_split, g + 1)
                        for m in range(2):
                            pe.wait_ge(relu_1, g * 16 + e * 2 + m + 1)
                            for k in range(KC):
                                mm = three(bank[m][:, 0:T], e, k, m, xh[:, par, k, 0:T], xl[:, par, k, 0:T], k == 0, k == KC - 1)
                            mm.then_inc(mm_1, 1)

                    def layer_2(e):
                        pe.wait_ge(split_1, g * 16 + e * 2 + 2 + 2)
                        for m in range(2):
                            pe.wait_ge(relu_2, g * 16 + e * 2 + m + 1)
                            for k in range(KC):
                                mm = three(bank[2 + m][:, 0:T], NE + e, k, m, h_hi[:, 0, e % 2, k, 0:T], h_lo[:, 0, e % 2, k, 0:T], k == 0, k == KC - 1)
                            mm.then_inc(mm_2, 1)

                    def layer_3(e):
                        if e == 0:
                            pe.wait_ge(c_gtf, g + 1)
                            pe.wait_ge(c_y, 2 * g + 2)
                            for m in range(KC):
                                M(bank[4 + m][:, 0:T], bo_sb[:, m * P:(m + 1) * P], gate_t[:, par, 0:T], start=True, stop=False)
                        pe.wait_ge(split_2, g * 16 + e * 2 + 2 + C2)
                        for m in range(KC):
                            for k in range(KC):
                                mm = three(bank[4 + m][:, 0:T], 2 * NE + e, k, m, h_hi[:, 1, e % 2, k, 0:T], h_lo[:, 1, e % 2, k, 0:T],
                                           False, e == NE - 1 and k == KC - 1)
                        mm.then_inc(mm_3, 1)

                    for e in range(NE + 2):
                        if e < NE:
                            layer_1(e)
                        if 1 <= e <= NE:
                            layer_2(e - 1)
                        if e >= 2:
                            layer_3(e - 2)
                        if nxt and e == 4:
                            turn(g + 1, nxt, 1 - par)
                        if nxt and e == 5:
                            logits(g + 1, nxt, 1 - par)
                        if nxt and e == 7:
                            turn_gates(g + 1, nxt, 1 - par)
                    pe.wait_ge(c_y, 2 * g + 4)
                    if nxt:
                        pe.wait_ge(c_gtf, g + 2)
                    for j in range(nb):
                        for m in range(KC):
                            mm = nc.tensor.transpose(bank[6 + j // 2][:, (j % 2 * KC + m) * P:(j % 2 * KC + m + 1) * P],
                                                     y_t[:, m, j * P:(j + 1) * P], ident[:])
                    mm.then_inc(c_yt, 1)

                def first(g, nb, par):
                    turn(g, nb, par)
                    logits(g, nb, par)
                    turn_gates(g, nb, par)

                groups(pe, first, body)

            @block.scalar
            def _(act):
                A = nc.scalar.activation
                act.sem_inc(relu_1, 2)
                act.sem_inc(relu_2, 2)
                act.sem_inc(c_y, 2)

                def norm(g, nb, par):
                    act.wait_ge(c_var, g + 1)
                    A(sd3[:, 0:nb], var3[:, 0:nb], ACT.Sqrt).then_inc(c_sd, 1)

                def turned(g, nb, par):
                    act.wait_ge(c_xt, g + 1)
                    for k in range(KC):
                        nc.scalar.copy(xt_f[:, k, 0:nb * P], bank[6 + k][:, 0:nb * P]).then_inc(c_xtf, 1)

                def exps(g, nb, par):
                    act.wait_ge(c_sub, g + 1)
                    A(lexp[:, 0:nb, :], lg[:, 0:nb, :], ACT.Exp).then_inc(c_exp, 1)

                def gates(g, nb, par):
                    act.wait_ge(c_gt, g + 1)
                    if not (isinstance(g, int) and g == 0):
                        act.wait_ge(c_gout, 16 * g)
                    nc.scalar.copy(gate_t[:, par, 0:nb * P], bank[7][0:NE, 0:nb * P]).then_inc(c_gtf, 1)

                def body(g, nb, par, nxt):
                    T = nb * P

                    def relu(layer, e, mm, ready, split, more):
                        for m in range(2):
                            n = g * 16 + e * 2 + m + 1
                            act.wait_ge(mm, n)
                            act.wait_ge(split, n + more)
                            A(h_f[:, layer, m, 0:T], bank[2 * layer + m][:, 0:T], ACT.Relu,
                              bias=bn_c[:, layer, 2 * e + m:2 * e + m + 1], scale=bn_s[:, layer, 2 * e + m:2 * e + m + 1]).then_inc(ready, 1)

                    for e in range(NE + 1):
                        if e < NE:
                            relu(0, e, mm_1, relu_1, split_1, 0)
                        if e >= 1:
                            relu(1, e - 1, mm_2, relu_2, split_2, C2 - 2)
                        if nxt and e == 2:
                            norm(g + 1, nxt, 1 - par)
                        if nxt and e == 4:
                            turned(g + 1, nxt, 1 - par)
                        if nxt and e == 6:
                            exps(g + 1, nxt, 1 - par)
                        if nxt and e == 8:
                            gates(g + 1, nxt, 1 - par)
                    act.wait_ge(mm_3, (g + 1) * NE + 2)
                    act.wait_ge(c_yt, g + 1)
                    for m in range(KC):
                        nc.scalar.copy(y_t[:, m, 0:T], bank[4 + m][:, 0:T]).then_inc(c_y, 1)

                
                def first(g, nb, par):
                    norm(g, nb, par)
                    turned(g, nb, par)
                    exps(g, nb, par)
                    gates(g, nb, par)

                groups(act, first, body)

            @block.vector
            def _(dve):
                V = nc.vector
                base = [None, 0, 0]

                def link(ins):
                    base[1] += 1
                    ins.then_inc(dve_c, 1)
                    dve.wait_ge(dve_c, base[0] + base[1])

                dve.sem_inc(split_1, 2)
                dve.sem_inc(split_2, C2)
                dve.sem_inc(c_fin, 2)
                base[0] = 0
                a_sum, r_sum = accv[:, :, D], accv[:, :, D + 1]
                link(V.tensor_tensor(a_sum, a_sum, r_sum, ALU.add))
                link(V.tensor_scalar(a_sum, a_sum, DEN_EPS, None, ALU.add))
                link(V.reciprocal(a_sum, a_sum))
                link(V.tensor_tensor(r_sum, r_sum, a_sum, ALU.mult))

                def residual(g, nb, par, stage):
                    a = [accv[:, at_block(g, j), 0:D].rearrange("p b d -> p (b d)") for j in range(nb)]
                    column = lambda j, c: accv[:, at_block(g, j), c:c + 1].rearrange("p b d -> p (b d)")
                    if stage == 0:
                        dve.wait_ge(c_in, 32 * (g + 1))
                        for j in range(nb):
                            last = V.scalar_tensor_tensor(out=a[j], in0=a[j], scalar=column(j, D), in1=xg[:, j, :], op0=ALU.mult, op1=ALU.add)
                        link(last)
                    if stage == 1:
                        for j in range(nb):
                            last = V.scalar_tensor_tensor(out=a[j], in0=xng[:, j, :], scalar=column(j, D + 1), in1=a[j], op0=ALU.mult, op1=ALU.add)
                        link(last)
                        V.memset(var3[:, 0:1], 0.0)
                    if stage == 2:
                        for j in range(nb):
                            last = V.bn_stats(st3[:, j, :], a[j])
                        link(last)
                        V.memset(var3[:, 0:1], 0.0)
                        for j in range(nb):
                            last = V.bn_aggr(mv3[:, j, :], st3[:, j, :])
                        link(last)
                        V.tensor_scalar(var3[:, 0:nb], mv3[:, 0:nb, 1], LN_EPS, None, ALU.add).then_inc(c_var, 1)

                def norm(g, nb, par):
                    dve.wait_ge(c_sd, g + 1)
                    link(V.reciprocal(rs3[:, 0:nb], sd3[:, 0:nb]))
                    for j in range(nb):
                        last = V.tensor_scalar(xg[:, j, :], accv[:, at_block(g, j), 0:D].rearrange("p b d -> p (b d)"),
                                               mv3[:, j, 0:1], rs3[:, j:j + 1], ALU.subtract, ALU.mult)
                    last.then_inc(c_xhat, 1)

                def split_x(g, nb, par):
                    dve.wait_ge(c_xtf, 2 * (g + 1))
                    T = nb * P
                    link(V.tensor_copy(xh[:, par, :, 0:T], xt_f[:, :, 0:T]))
                    V.tensor_tensor(xl[:, par, :, 0:T], xt_f[:, :, 0:T], xh[:, par, :, 0:T].bitcast(F32), ALU.subtract).then_inc(c_split, 1)

                def softmax_1(g, nb, par):
                    dve.wait_ge(c_lg, g + 1)
                    l = lg[:, 0:nb, :]
                    link(V.tensor_tensor(l, bank[6][:, 0:nb * NE].rearrange("p (b e) -> p b e", e=NE),
                                         br_sb[:].unsqueeze(1).broadcast_to([P, nb, NE]), ALU.add))
                    link(V.tensor_reduce(lmax[:, 0:nb], l, AX.X, ALU.max))
                    V.tensor_tensor(l, l, lmax[:, 0:nb].unsqueeze(2).broadcast_to([P, nb, NE]), ALU.subtract).then_inc(c_sub, 1)

                def softmax_2(g, nb, par):
                    dve.wait_ge(c_exp, g + 1)
                    link(V.tensor_reduce(lmax[:, 0:nb], lexp[:, 0:nb, :], AX.X, ALU.add))
                    link(V.reciprocal(lmax[:, 0:nb], lmax[:, 0:nb]))
                    V.tensor_tensor(gate[:, 0:nb, :], lexp[:, 0:nb, :], lmax[:, 0:nb].unsqueeze(2).broadcast_to([P, nb, NE]), ALU.mult).then_inc(c_gate, 1)

                def body(g, nb, par, nxt):
                    T = nb * P

                    def split_1_(e):
                        for m in range(2):
                            n = g * 16 + e * 2 + m
                            dve.wait_ge(relu_1, n + 3)
                            hi = h_hi[:, 0, e % 2, m, 0:T]
                            link(V.tensor_copy(hi, h_f[:, 0, m, 0:T]))
                            V.tensor_tensor(h_lo[:, 0, e % 2, m, 0:T], h_f[:, 0, m, 0:T], hi.bitcast(F32), ALU.subtract).then_inc(split_1, 1)

                    def split_2_(e):
                        for m in range(2):
                            n = g * 16 + e * 2 + m
                            dve.wait_ge(relu_2, n + 3)
                            if m == 0:
                                dve.wait_ge(c_bc[e % NW], (g * 2 + e // NW + 1) * 16)
                                dve.wait_ge(mm_3, g * NE + e + 1)
                            link(V.tensor_tensor(h_f[:, 1, m, 0:T], h_f[:, 1, m, 0:T], gate_bc[:, e % NW, 0:T], ALU.mult))
                            hi = h_hi[:, 1, e % 2, m, 0:T]
                            link(V.tensor_copy(hi, h_f[:, 1, m, 0:T]))
                            V.tensor_tensor(h_lo[:, 1, e % 2, m, 0:T], h_f[:, 1, m, 0:T], hi.bitcast(F32), ALU.subtract).then_inc(split_2, 1)

                    for e in range(NE + 1):
                        if e < NE:
                            split_1_(e)
                        if e >= 1:
                            split_2_(e - 1)
                        if nxt and e < 3:
                            residual(g + 1, nxt, 1 - par, e)
                        if nxt and e == 3:
                            norm(g + 1, nxt, 1 - par)
                        if nxt and e == 5:
                            split_x(g + 1, nxt, 1 - par)
                        if nxt and e == 6:
                            softmax_1(g + 1, nxt, 1 - par)
                        if nxt and e == 7:
                            softmax_2(g + 1, nxt, 1 - par)
                    dve.wait_ge(c_yt, g + 2)
                    for j in range(nb):
                        a = accv[:, at_block(g, j), 0:D].rearrange("p b d -> p (b d)")
                        last = V.tensor_tensor(a, a, bank[6 + j // 2][:, j % 2 * D:(j % 2 + 1) * D], ALU.add)
                    last.then_inc(c_fin, 1)

                for stage in range(3):
                    residual(0, GB, 0, stage)
                norm(0, GB, 0)
                split_x(0, GB, 0)
                softmax_1(0, GB, 0)
                softmax_2(0, GB, 0)
                ahead = base[1]
                LINKS = 4 + 1 + 1 + 2 + 2 + 2 * NE + 4 * NE
                with dve.Fori(0, ITC) as it:
                    base[0], base[1] = it * (2 * LINKS) + ahead, 0
                    body(it * 2, GB, 0, GB)
                    body(it * 2 + 1, GB, 1, GB)
                    assert base[1] == 2 * LINKS, base[1]
                base[0], base[1] = ahead + ITC * 2 * LINKS, 0
                for n, (g, nb) in enumerate(GRP):
                    body(g, nb, g % 2, GRP[n + 1][1] if n + 1 < len(GRP) else 0)


_BN1 = ["L0_ffn_b1", "L0_ffn_g1", "L0_ffn_be1", "L0_ffn_m1", "L0_ffn_v1"]
_BN2 = ["L0_ffn_b2", "L0_ffn_g2", "L0_ffn_be2", "L0_ffn_m2", "L0_ffn_v2"]
_INS = ["x", "src", "dst", "L0_gnn_W_dis", "L0_ffn_Wr", "L0_ffn_br", *_BN1, *_BN2, "L0_ffn_W1", "L0_ffn_W2", "L0_ffn_Wo", "L0_ffn_bo"]


def kernel(**inputs):
    import numpy as np
    import concourse.bacc as bacc
    from concourse import mybir as mb
    from concourse.bass_utils import run_bass_kernel_spmd

    nc = bacc.Bacc("TRN2", target_bir_lowering=False, num_devices=1)
    arrays, a = {}, {}
    for name in _INS:
        v = np.ascontiguousarray(inputs[name])
        arrays[f"in_{name}"] = v
        a[name] = nc.dram_tensor(f"in_{name}", v.shape, mb.dt.from_np(v.dtype), kind="ExternalInput").ap()
    out = nc.dram_tensor("out", arrays["in_x"].shape, mb.dt.float32, kind="ExternalOutput").ap()
    graph_mixture(nc, a["x"], a["src"], a["dst"], a["L0_gnn_W_dis"], a["L0_ffn_Wr"], a["L0_ffn_br"],
                  [a[n] for n in _BN1], [a[n] for n in _BN2], a["L0_ffn_W1"], a["L0_ffn_W2"], a["L0_ffn_Wo"], a["L0_ffn_bo"], out)
    r = run_bass_kernel_spmd(nc, [arrays], core_ids=[0])
    return r.results[0]["out"]
```

```python
from contextlib import ExitStack

import concourse.bass as bass
from concourse import mybir
from concourse.alu_op_type import AluOpType as ALU

ACT = mybir.ActivationFunctionType
AX = mybir.AxisListType
F32 = mybir.dt.float32
F32R = mybir.dt.float32r
BF16 = mybir.dt.bfloat16
I32 = mybir.dt.int32
DVE_ENGINE = mybir.EngineType.DVE
PE_ENGINE = mybir.EngineType.PE

P = 128


def graph_mixture(nc, x, src, dst, w_dis, wr, br, bn1, bn2, w1, w2, wo, bo, out):
    N, D = x.shape
    E = src.shape[0]
    Q = w_dis.shape[0]
    NE = wr.shape[1]
    KC = D // P
    NB = -(-N // P)
    TAIL = N - (NB - 1) * P
    NT = -(-E // P)
    TC = -(-NT // P)
    FULL = (TC - 1) * P
    LAST = NT - 1 - FULL
    ETAIL = E - (NT - 1) * P
    SB = 8
    UN = 2
    STEPS = -(-(NT + NB - 1) // (SB * UN)) * SB * UN
    NBATCH = STEPS // SB
    SH = STEPS // 2
    ROW = D + Q
    MW = D + 2
    LN_EPS, BN_EPS, DEN_EPS = 1e-5, 1e-3, 0.01
    MID = (NB // 2) * P
    PAD = float(1 << 20)
    GB = 3
    NG = (NB - 4) // GB + 2
    SIZE = [2] + [GB] * (NG - 2) + [2]
    TOK = GB * P
    LC = 8
    CH = (NB - 1) // LC
    assert max(MID, N - MID) <= 1 << 12 and STEPS + NB <= 1 << 12
    assert SH <= 512 and sum(SIZE) == NB and (NB - 1) % (2 * LC) == 0

    xn_table = nc.dram_tensor("xn_table", [NB * P, ROW], F32)
    dst_rows = nc.dram_tensor("dst_rows", [NBATCH, SB * P], BF16)
    gate_rows = nc.dram_tensor("gate_rows", [NE, NB * P + 2 * P], F32)
    table_ap, rows_ap, gates_ap = xn_table.ap(), dst_rows.ap(), gate_rows.ap()

    top, graph = ExitStack(), ExitStack()
    with top:
        def sem(name):
            return top.enter_context(nc.semaphore(name))

        def sb(ctx, name, shape, dt):
            return ctx.enter_context(nc.sbuf_tensor(name, shape, dt, side="right" if ctx is graph else "left"))

        bank = [top.enter_context(nc.psum_tensor(f"bank{i}", [P, 512], F32)) for i in range(8)]

        wh = sb(top, "wh", [P, 3 * NE, KC * D], F32R)
        wl = sb(top, "wl", [P, 3 * NE, KC * D], F32R)
        ident = sb(top, "ident", [P, P], F32)
        bn_s = sb(top, "bn_s", [P, 2, 2 * NE], F32)
        bn_c = sb(top, "bn_c", [P, 2, 2 * NE], F32)
        wr_sb = sb(top, "wr_sb", [P, KC, NE], F32)
        br_sb = sb(top, "br_sb", [P, NE], F32)
        bo_s = sb(top, "bo_s", [64 + NE, D], F32R)

        top.enter_context(graph)
        src_step = sb(graph, "src_step", [P, NBATCH, SB], I32)
        dst_step = sb(graph, "dst_step", [P, NBATCH, SB], F32)
        q_parts = sb(graph, "q_parts", [P, NB * 3 * Q], BF16)
        at = sb(graph, "at", [P, NBATCH, SB], I32)
        acc_at, q_at = at[0:1], at[32:33]
        many = sb(graph, "many", [P, 1], I32)
        iota = sb(graph, "iota", [P, P], F32)
        lane = sb(graph, "lane", [P, 1], F32)

        with ExitStack() as pa:
            x_tile = sb(pa, "x_tile", [P, 2, LC, D], F32)
            xnq = sb(pa, "xnq", [P, 2, LC, ROW], F32)
            raw2 = sb(pa, "raw2", [P, 2, KC * D], F32)
            late = xnq[:].rearrange("p a b r -> p (a b r)")[:, 2 * LC * ROW - 4 * KC * D:]
            raw = [raw2[:, 0, :], raw2[:, 1, :]] + [late[:, n * KC * D:(n + 1) * KC * D] for n in range(4)]
            assert 4 * KC * D <= LC * ROW
            RB = len(raw)
            iota_s = sb(pa, "iota_s", [P, STEPS], F32)
            ones = sb(pa, "ones", [P, P], F32)
            tri = sb(pa, "tri", [P, P], F32)
            dst_i = sb(pa, "dst_i", [P, TC, P], I32)
            src_i = sb(pa, "src_i", [P, TC, P], I32)
            dst_f = sb(pa, "dst_f", [P, TC, P], F32)
            dst_r = sb(pa, "dst_r", [P, TC, P], F32R)
            src_r = sb(pa, "src_r", [P, TC, P], F32R)
            blk_i = sb(pa, "blk_i", [P, 2, TC], I32)
            blk_j = sb(pa, "blk_j", [P, 2, TC], I32)
            blk_f = sb(pa, "blk_f", [P, 2, TC], F32)
            npair = sb(pa, "npair", [P, TC], F32)
            pref = sb(pa, "pref", [P, 2, TC], F32)
            scan = sb(pa, "scan", [P, TC], F32)
            zero = sb(pa, "zero", [P, TC], F32)
            t_st = sb(pa, "t_st", [P, TC], F32)
            t_en = sb(pa, "t_en", [P, TC], F32)
            t_fs = sb(pa, "t_fs", [P, TC], F32R)
            below = sb(pa, "below", [P, STEPS], F32)
            sels = sb(pa, "sels", [P, 2, STEPS], F32R)
            dclamp = sb(pa, "dclamp", [P, TC * P], F32)
            dpos = dclamp[:].rearrange("p (c e) -> p c e", e=P)
            rows_sb = sb(pa, "rows_sb", [P, TC, P], BF16)
            bo_sb = sb(pa, "bo_sb", [NE, D], F32)
            wd_in = sb(pa, "wd_in", [Q, D], F32)
            wd_t = sb(pa, "wd_t", [P, KC, Q], F32)
            par_in = [t[0:2 * NE, n, :].bitcast(F32) for t in (dst_i, src_i) for n in range(5)]
            par = sb(pa, "par", [P, 10, 2 * NE], F32)
            xt = sb(pa, "xt", [P, 2, KC * P], F32)
            stats = sb(pa, "stats", [P, LC, 6], F32)
            mv = sb(pa, "mv", [P, LC, 2], F32)
            var = sb(pa, "var", [P, LC], F32)
            sd = sb(pa, "sd", [P, LC], F32)
            rstd = sb(pa, "rstd", [P, LC], F32)
            qr = sb(pa, "qr", [P, LC * Q], F32)
            qr2 = sb(pa, "qr2", [P, LC * Q], F32)
            bn_v = sb(pa, "bn_v", [P, 2, 2 * NE], F32)
            bn_d = sb(pa, "bn_d", [P, 2, 2 * NE], F32)

            edges_in, small_in, x_in = sem("edges_in"), sem("small_in"), [sem("x_in0"), sem("x_in1")]
            tail_cleared = sem("tail_cleared")
            raw_in = [sem(f"raw_in{n}") for n in range(RB)]
            hi_done, lo_done = sem("hi_done"), sem("lo_done")
            cleared, consts = sem("cleared"), sem("consts")
            dve_a, pool_a = sem("dve_a"), sem("pool_a")
            n_ready, pref_done = sem("n_ready"), sem("pref_done")
            dprime, sel_ready, sel_used = sem("dprime"), sem("sel_ready"), sem("sel_used")
            evac, rowt_done, rowt_copied, rows_out = sem("evac"), sem("rowt_done"), sem("rowt_copied"), sem("rows_out")
            part_done, bn_var, bn_sd = sem("part_done"), sem("bn_var"), sem("bn_sd")
            var_ready, sd_ready, xn_ready = sem("var_ready"), sem("sd_ready"), sem("xn_ready")
            xt_done, xt_copied, q_done, q_copied = sem("xt_done"), sem("xt_copied"), sem("q_done"), sem("q_copied")
            table_out, xnq_free = [sem("table_out0"), sem("table_out1")], sem("xnq_free")

            def chunks(eng, body):
                with eng.Fori(0, CH // 2) as it:
                    body(it * 2, LC, 0)
                    body(it * 2 + 1, LC, 1)
                body(CH, 1, 0)

            block = pa.enter_context(nc.Block())

            @block.sync
            def _(sp):
                sp.wait_ge(cleared, 2)
                for a, t in ((dst, dst_i), (src, src_i)):
                    sp.dma_start(t[:, 0:TC - 1, :], a[0:FULL * P].rearrange("(c p e) -> p c e", p=P, e=P)).then_inc(edges_in, 16)
                    sp.dma_start(t[0:LAST, TC - 1, :], a[FULL * P:(NT - 1) * P].rearrange("(p e) -> p e", e=P)).then_inc(edges_in, 16)
                    sp.dma_start(t[LAST:LAST + 1, TC - 1, 0:ETAIL], a[(NT - 1) * P:E].rearrange("(p e) -> p e", p=1)).then_inc(edges_in, 16)
                sp.dma_start(wd_in[:], w_dis).then_inc(small_in, 16)
                sp.dma_start(wr_sb[:], wr.rearrange("(k p) e -> p k e", p=P)).then_inc(small_in, 16)
                sp.dma_start(br_sb[:], br.partition_broadcast(P)).then_inc(small_in, 16)
                sp.dma_start(bo_sb[:], bo).then_inc(small_in, 16)

                def load_x(c, par):
                    sp.dma_start(x_tile[:, par], x[bass.ds(c * (LC * P), LC * P), :].rearrange("(b p) d -> p b d", p=P)).then_inc(x_in[par], 16)

                def load_w(n):
                    if n >= RB:
                        sp.wait_ge(lo_done, n - RB + 1)
                    sp.dma_start(raw[n % RB].rearrange("p (k h) -> p k h", k=KC),
                                 (w1, w2, wo)[n // NE][n % NE].rearrange("(k p) h -> p k h", p=P)).then_inc(raw_in[n % RB], 16)

                for n in range(RB):
                    load_w(n)
                load_x(0, 0)
                for n in range(RB, 3 * NE):
                    if n == RB + 4:
                        sp.wait_ge(n_ready, 1)
                        for m, a in enumerate((*bn1, *bn2)):
                            sp.dma_start(par_in[m], a.rearrange("e (m p) -> (e m) p", p=P)).then_inc(small_in, 16)
                    if n == 3 * NE - RB:
                        load_x(1, 1)
                    load_w(n)
                with sp.Fori(1, CH // 2) as it:
                    for par_ in range(2):
                        sp.wait_ge(xn_ready, it * 2 + par_ - 1)
                        load_x(it * 2 + par_, par_)
                sp.wait_ge(tail_cleared, 1)
                sp.dma_start(x_tile[0:TAIL, 0, 0, :], x[(NB - 1) * P:N, :]).then_inc(x_in[0], 16)
                sp.wait_ge(rowt_copied, -(-TC // 4))
                flat = rows_ap.rearrange("k (s e) -> (k s) e", e=P)
                whole = STEPS // P
                sp.dma_start(flat[0:whole * P, :].rearrange("(c p) e -> p c e", p=P), rows_sb[:, 0:whole, :]).then_inc(rows_out, 16)
                sp.dma_start(flat[whole * P:STEPS, :], rows_sb[0:STEPS - whole * P, whole, :]).then_inc(rows_out, 16)
                sp.wait_ge(rows_out, 32)

            @block.gpsimd
            def _(pool):
                pool.sem_inc(xnq_free, 2)
                nc.gpsimd.memset(dst_i[:, TC - 1, :], -int(PAD)).then_inc(cleared, 1)
                nc.gpsimd.memset(src_i[:, TC - 1, :], 0).then_inc(cleared, 1)
                nc.gpsimd.memset(ones[:], 1.0).then_inc(pool_a, 1)
                nc.gpsimd.memset(zero[:], 0.0).then_inc(pool_a, 1)
                pool.wait_ge(pool_a, 1)
                nc.gpsimd.affine_select(out=ident[:], in_=ones[:], compare_op=ALU.is_equal, fill=0.0, base=0,
                                        pattern=[[-1, P]], channel_multiplier=1).then_inc(consts, 1)
                nc.gpsimd.affine_select(out=tri[:], in_=ones[:], compare_op=ALU.is_gt, fill=0.0, base=0,
                                        pattern=[[1, P]], channel_multiplier=-1).then_inc(consts, 1)
                nc.gpsimd.iota(iota_s[:], pattern=[[1, STEPS]], base=0, channel_multiplier=0,
                               allow_small_or_imprecise_dtypes=True).then_inc(consts, 1)
                nc.gpsimd.iota(iota[:], pattern=[[1, P]], base=0, channel_multiplier=0,
                               allow_small_or_imprecise_dtypes=True).then_inc(consts, 1)
                nc.gpsimd.iota(lane[:], pattern=[[0, 1]], base=0, channel_multiplier=1,
                               allow_small_or_imprecise_dtypes=True).then_inc(consts, 1)
                for n in range(3 * NE):
                    pool.wait_ge(hi_done, n + 1)
                    nc.gpsimd.tensor_tensor(out=wl[:, n, :], in0=raw[n % RB], in1=wh[:, n, :].bitcast(F32),
                                            op=ALU.subtract).then_inc(lo_done, 1)

                def rows_out_(c, nb, par_):
                    pool.wait_ge(q_copied, c + 1)
                    pool.dma_start(table_ap[bass.ds(c * (LC * P), nb * P), :].rearrange("(b p) r -> p b r", p=P),
                                   xnq[:, par_, 0:nb, :]).then_inc(table_out[par_], 16)

                def left(c, par_):
                    pool.wait_ge(table_out[par_], (c - par_) * 8 + 16)
                    pool.sem_inc(xnq_free, 1)

                with pool.Fori(0, CH // 2 - 1) as it:
                    for par_ in range(2):
                        rows_out_(it * 2 + par_, LC, par_)
                        left(it * 2 + par_, par_)
                rows_out_(CH - 2, LC, 0)
                left(CH - 2, 0)
                rows_out_(CH - 1, LC, 1)
                rows_out_(CH, 1, 0)
                pool.wait_ge(table_out[1], CH // 2 * 16)
                pool.wait_ge(table_out[0], (CH // 2 + 1) * 16)

            @block.scalar
            def _(act):
                def deviations(c):
                    act.wait_ge(var_ready, c + 1)
                    nc.scalar.activation(sd[:], var[:], ACT.Sqrt).then_inc(sd_ready, 1)

                for n in range(3 * NE):
                    if n == 3 * NE - 6:
                        deviations(0)
                    act.wait_ge(raw_in[n % RB], 16 * (n // RB + 1))
                    nc.scalar.copy(wh[:, n, :], raw[n % RB]).then_inc(hi_done, 1)

                def body(c, nb, par_):
                    for j in range(nb):
                        act.wait_ge(xt_done, c * LC + j + 1)
                        nc.scalar.copy(xt[:, j % 2, :], bank[j % 2][:, 0:KC * P]).then_inc(xt_copied, 1)
                        if j == LC - 4:
                            deviations(c + 1)
                    act.wait_ge(q_done, c * LC + nb)
                    nc.scalar.mul(xnq[:, par_, 0:nb, D:ROW], bank[2][:, 0:nb * Q].rearrange("p (b q) -> p b q", q=Q), 0.25).then_inc(q_copied, 1)

                act.wait_ge(bn_var, 1)
                nc.scalar.activation(bn_d[:], bn_v[:], ACT.Sqrt).then_inc(bn_sd, 1)
                chunks(act, body)

            @block.tensor
            def _(pe):
                pe.wait_ge(consts, 2)
                pe.wait_ge(n_ready, 1)
                nc.tensor.matmul(bank[6][:, 0:TC], tri[:], npair[:], start=True, stop=True)
                nc.tensor.matmul(bank[6][:, TC:2 * TC], ones[:], npair[:], start=True, stop=True).then_inc(pref_done, 1)
                pe.wait_ge(dprime, 1)
                for c in range(TC):
                    pe.wait_ge(sel_ready, c + 1)
                    for n, lhs in enumerate((src_r[:, c, :], dst_r[:, c, :], t_fs[:, c:c + 1].broadcast_to([P, P]))):
                        for h in range(2):
                            mm = nc.tensor.matmul(bank[2 * n + h][:, 0:SH], lhs, sels[:, c % 2, h * SH:(h + 1) * SH],
                                                  start=(c == 0), stop=(c == TC - 1))
                    mm.then_inc(sel_used, 1)
                pe.wait_ge(small_in, 16 * 14)
                for n in range(10):
                    nc.tensor.transpose(bank[7][:, n * 2 * NE:(n + 1) * 2 * NE], par_in[n], ident[0:2 * NE, 0:2 * NE])
                for k in range(KC):
                    mm = nc.tensor.transpose(bank[7][:, 160 + k * Q:160 + (k + 1) * Q], wd_in[:, k * P:(k + 1) * P], ident[0:Q, 0:Q])
                mm.then_inc(part_done, 1)
                pe.wait_ge(evac, 1)
                pe.wait_ge(bn_var, 1)
                for c in range(TC):
                    nc.tensor.transpose(bank[6 + c // 4][:, c % 4 * P:(c % 4 + 1) * P], dclamp[:, c * P:(c + 1) * P], ident[:]).then_inc(rowt_done, 1)
                def body(c, nb, par_):
                    pe.wait_ge(xn_ready, c + 1)
                    for j in range(nb + 1):
                        if j < nb:
                            if j >= 2:
                                pe.wait_ge(xt_copied, c * LC + j - 1)
                            for k in range(KC):
                                mm = nc.tensor.transpose(bank[j % 2][:, k * P:(k + 1) * P], xnq[:, par_, j, k * P:(k + 1) * P], ident[:])
                            mm.then_inc(xt_done, 1)
                        if j >= 1:
                            pe.wait_ge(xt_copied, c * LC + j)
                            for k in range(KC):
                                mm = nc.tensor.matmul(bank[2][:, (j - 1) * Q:j * Q], xt[:, (j - 1) % 2, k * P:(k + 1) * P], wd_t[:, k, :],
                                                      start=(k == 0), stop=(k == KC - 1))
                            mm.then_inc(q_done, 1)

                chunks(pe, body)

            @block.vector
            def _(dve):
                done = [0]

                def link(ins):
                    done[0] += 1
                    ins.then_inc(dve_a, 1)
                    dve.wait_ge(dve_a, done[0])

                V = nc.vector
                dve.wait_ge(edges_in, 96)
                V.tensor_copy(dst_f[:], dst_i[:])
                link(V.tensor_scalar(src_r[:], src_i[:], -float(MID), None, ALU.add))
                V.tensor_scalar(dst_r[:], dst_f[:], -float(MID), None, ALU.add)
                link(V.tensor_scalar(dpos, dst_f[:], 0.0, 2 * PAD, ALU.is_lt, ALU.mult))
                link(V.tensor_tensor(dpos, dpos, dst_f[:], ALU.add))
                V.tensor_reduce(blk_i[:, 0, :], dpos, AX.X, ALU.min)
                link(V.tensor_reduce(blk_i[:, 1, :], dst_f[:], AX.X, ALU.max))
                link(V.tensor_scalar(blk_j[:], blk_i[:], 7, None, ALU.arith_shift_right))
                link(V.tensor_copy(blk_f[:], blk_j[:]))
                link(V.tensor_scalar(blk_f[:, 1, :], blk_f[:, 1, :], -1.0, 1.0, ALU.max, ALU.add))
                link(V.tensor_tensor(npair[:], blk_f[:, 1, :], blk_f[:, 0, :], ALU.subtract))
                V.tensor_scalar(npair[:], npair[:], 0.0, None, ALU.max).then_inc(n_ready, 1)
                dve.wait_ge(pref_done, 1)
                dve.wait_ge(pool_a, 2)
                link(V.tensor_copy(pref[:].rearrange("p a c -> p (a c)"), bank[6][:, 0:2 * TC]))
                link(V.tensor_tensor_scan(scan[:], pref[:, 1, :], zero[:], 0.0, ALU.add, ALU.add))
                link(V.tensor_scalar(many[:], scan[:, TC - 1:TC], float(STEPS), None, ALU.is_gt))
                link(V.tensor_tensor(scan[:], scan[:], pref[:, 1, :], ALU.subtract))
                link(V.tensor_tensor(t_st[:], scan[:], pref[:, 0, :], ALU.add))
                V.scalar_tensor_tensor(out=t_fs[:], in0=blk_f[:, 0, :], scalar=-float(MID // P), in1=t_st[:],
                                       op0=ALU.add, op1=ALU.subtract).then_inc(dprime, 1)
                link(V.tensor_tensor(t_en[:], t_st[:], npair[:], ALU.add))
                dve.wait_ge(consts, 5)
                for c in range(TC):
                    if c >= 1:
                        dve.wait_ge(sel_ready, c)
                    link(V.tensor_scalar(below[:], iota_s[:], t_en[:, c:c + 1], None, ALU.is_lt))
                    if c >= 2:
                        dve.wait_ge(sel_used, c - 1)
                    V.scalar_tensor_tensor(out=sels[:, c % 2, :], in0=iota_s[:], scalar=t_st[:, c:c + 1], in1=below[:],
                                           op0=ALU.is_ge, op1=ALU.mult).then_inc(sel_ready, 1)
                per = 8
                base = done[0]
                here = [0, 0]

                def link_c(ins):
                    here[1] += 1
                    ins.then_inc(dve_a, 1)
                    dve.wait_ge(dve_a, here[0] + here[1])

                def statistics(c, nb, par_):
                    dve.wait_ge(x_in[par_], (c - par_) * 8 + 16)
                    for j in range(nb):
                        last = V.bn_stats(stats[:, j, :], x_tile[:, par_, j, :])
                    link_c(last)
                    V.memset(scan[:, 0:1], 0.0)
                    for j in range(nb):
                        last = V.bn_aggr(mv[:, j, :], stats[:, j, :])
                    link_c(last)
                    V.tensor_scalar(var[:, 0:nb], mv[:, 0:nb, 1], LN_EPS, None, ALU.add).then_inc(var_ready, 1)

                def normed(c, nb, par_):
                    dve.wait_ge(sd_ready, c + 1)
                    link_c(V.reciprocal(rstd[:, 0:nb], sd[:, 0:nb]))
                    dve.wait_ge(xnq_free, c + 1)
                    for j in range(nb):
                        last = V.tensor_scalar(xnq[:, par_, j, 0:D], x_tile[:, par_, j, :], mv[:, j, 0:1], rstd[:, j:j + 1], ALU.subtract, ALU.mult)
                    last.then_inc(xn_ready, 1)

                def norm(c, nb, par_):
                    statistics(c, nb, par_)
                    normed(c, nb, par_)

                def split_q(c, nb, par_):
                    dve.wait_ge(q_copied, c + 1)
                    qv = xnq[:, par_, 0:nb, D:ROW]
                    qp = q_parts[:, bass.ds(c * (LC * 3 * Q), nb * 3 * Q)].rearrange("p (b t q) -> p b t q", t=3, q=Q)
                    q1 = qr[:, 0:nb * Q].rearrange("p (b q) -> p b q", q=Q)
                    q2 = qr2[:, 0:nb * Q].rearrange("p (b q) -> p b q", q=Q)
                    link_c(V.tensor_copy(qp[:, :, 0, :], qv))
                    link_c(V.tensor_tensor(q1, qv, qp[:, :, 0, :], ALU.subtract))
                    link_c(V.tensor_copy(qp[:, :, 1, :], q1))
                    link_c(V.tensor_tensor(q2, q1, qp[:, :, 1, :], ALU.subtract))
                    link_c(V.tensor_copy(qp[:, :, 2, :], q2))
                    if nb == 1:
                        return
                    assert here[1] % per == 0, here

                here[0] = base
                statistics(0, LC, 0)
                base += here[1]
                done[0] = base
                dve.wait_ge(sel_used, TC)
                srcv, dstv = (t[:].rearrange("p k s -> p (k s)") for t in (src_step, dst_step))
                atall = at[:].rearrange("p k s -> p (k s)")
                halves = [slice(h * SH, (h + 1) * SH) for h in range(2)]
                for h, cols in enumerate(halves):
                    last = V.tensor_tensor(below[:, cols], iota_s[:, cols], bank[4 + h][:, 0:SH], ALU.add)
                link(last)
                for h, cols in enumerate(halves):
                    V.tensor_scalar(srcv[:, cols], bank[0 + h][:, 0:SH], float(MID), None, ALU.add)
                    last = V.scalar_tensor_tensor(out=dstv[:, cols], in0=below[:, cols], scalar=-float(P), in1=bank[2 + h][:, 0:SH],
                                                  op0=ALU.mult, op1=ALU.add)
                link(last)
                link(V.tensor_scalar(below[0:33, :], below[0:33, :], -float(MID // P), float(NB - 1 - MID // P), ALU.max, ALU.min))
                V.tensor_scalar(atall[0:1, :], below[0:1, :], float(MID // P), float(MW), ALU.add, ALU.mult)
                V.tensor_scalar(atall[32:33, :], below[32:33, :], float(MID // P), float(3 * Q), ALU.add, ALU.mult)
                V.memset(dclamp[:, STEPS:], -1.0)
                V.tensor_scalar(dclamp[:, 0:STEPS], dstv, -1.0, float(P), ALU.max, ALU.min).then_inc(evac, 1)
                dve.wait_ge(part_done, 1)
                V.tensor_copy(par[:].rearrange("p a b -> p (a b)"), bank[7][:, 0:160])
                link(V.tensor_copy(wd_t[:].rearrange("p k q -> p (k q)"), bank[7][:, 160:160 + KC * Q]))
                pv = par[:].rearrange("p (l n) m -> p l n m", l=2)
                V.tensor_scalar(bn_v[:], pv[:, :, 4, :], BN_EPS, None, ALU.add).then_inc(bn_var, 1)
                here[0], here[1] = done[0], 0
                normed(0, LC, 0)
                done[0] += here[1]
                for c in range(0, TC, 4):
                    nt = min(4, TC - c)
                    dve.wait_ge(rowt_done, c + nt)
                    V.tensor_copy(rows_sb[:, c:c + nt, :], bank[6 + c // 4][:, 0:nt * P].rearrange("p (c e) -> p c e", e=P)).then_inc(rowt_copied, 1)
                base = done[0]
                dve.wait_ge(lo_done, 3 * NE)
                with dve.Fori(0, CH // 2 - 1) as it:
                    here[0], here[1] = it * (2 * per) + base, 0
                    norm(it * 2 + 1, LC, 1)
                    split_q(it * 2, LC, 0)
                    norm(it * 2 + 2, LC, 0)
                    split_q(it * 2 + 1, LC, 1)
                base += 2 * per * (CH // 2 - 1)
                here[0], here[1] = base, 0
                V.memset(x_tile[:, 0, 0, :], 0.0).then_inc(tail_cleared, 1)
                norm(CH - 1, LC, 1)
                split_q(CH - 2, LC, 0)
                norm(CH, 1, 0)
                split_q(CH - 1, LC, 1)
                split_q(CH, 1, 0)
                base += here[1]
                dve.wait_ge(bn_sd, 1)
                link2 = [0]

                def link_e(ins):
                    link2[0] += 1
                    ins.then_inc(dve_a, 1)
                    dve.wait_ge(dve_a, base + link2[0])

                link_e(V.memset(bo_s[:].bitcast(F32), 0.0))
                link_e(V.tensor_copy(bo_s[0:NE], bo_sb[:]))
                V.tensor_copy(bo_s[32:32 + NE], bo_s[0:NE].bitcast(F32))
                V.tensor_tensor(bo_s[64:64 + NE], bo_sb[:], bo_s[0:NE].bitcast(F32), ALU.subtract)
                link_e(V.reciprocal(bn_v[:], bn_d[:]))
                link_e(V.tensor_tensor(bn_s[:], pv[:, :, 1, :], bn_v[:], ALU.mult))
                link_e(V.tensor_tensor(bn_c[:], pv[:, :, 0, :], pv[:, :, 3, :], ALU.subtract))
                link_e(V.tensor_tensor(bn_c[:], bn_c[:], bn_s[:], ALU.mult))
                V.tensor_tensor(bn_c[:], bn_c[:], pv[:, :, 2, :], ALU.add)


        acc = sb(top, "acc", [P, NB * MW], F32)

        with ExitStack() as pb:
            rows = sb(pb, "rows", [P, UN * SB * ROW], F32)
            index = sb(pb, "index", [P, UN, SB], I32)
            hot_t = sb(pb, "hot_t", [P, UN, SB * P], BF16)
            hot = sb(pb, "hot", [P, UN, SB, P], F32)
            e_sc = sb(pb, "e_sc", [P, UN, SB], F32)
            msg = sb(pb, "msg", [P, UN, SB, MW], F32)
            rowsv = rows[:].rearrange("p (u s r) -> p u s r", u=UN, s=SB)

            index_ready, gathered = sem("index_ready"), [sem(f"gathered{u}") for u in range(UN)]
            bc_in = [sem(f"bc_in{u}") for u in range(UN)]
            hot_t_ready, qd_done, weights_ready = sem("hot_t_ready"), sem("qd_done"), sem("weights_ready")
            hot_ready, msg_ready, product, added = sem("hot_ready"), sem("msg_ready"), sem("product"), sem("added")
            gather_turn, cleared_b, dve_b = sem("gather_turn"), sem("cleared_b"), sem("dve_b")
            ITERS = NBATCH // UN

            def batches(eng, body):
                with eng.Fori(0, ITERS - 1) as it:
                    k0, n0 = eng.snap(it * UN), eng.snap(it * (UN * SB))
                    for u in range(UN):
                        body(k0 + u, n0 + u * SB, u, UN)
                for u in range(UN):
                    k = (ITERS - 1) * UN + u
                    body(k, k * SB, u, UN - 1 - u)

            block = pb.enter_context(nc.Block())

            @block.sync
            def _(sp):
                with sp.Fori(0, ITERS) as it:
                    for u in range(UN):
                        k = it * UN + u
                        sp.wait_ge(qd_done, k + 1)
                        sp.dma_start(hot_t[:, u, :], rows_ap[bass.ds(k, 1), :].rearrange("a e -> (a e)").partition_broadcast(P)
                                     ).then_inc(bc_in[u], 16)

            @block.gpsimd
            def _(pool):
                with pool.Fori(0, ITERS) as it:
                    for u in range(UN):
                        k = it * UN + u
                        pool.wait_ge(index_ready, k + 1)
                        pool.sem_inc(gather_turn, 1)
                        for s in range(SB):
                            pool.indirect_dma_start(out=rowsv[:, u, s, :], out_offset=None, in_=table_ap,
                                                    in_offset=bass.IndirectOffsetOnAxis(ap=index[:, u, s:s + 1], axis=0)).then_inc(gathered[u], 16)

            @block.tensor
            def _(pe):
                def q_of_destinations(k, u):
                    pe.wait_ge(hot_t_ready, k + 1)
                    pe.wait_ge(weights_ready, k + 1)
                    _, at = nc.values_load_multi_w_load_instructions(
                        q_at[:, bass.ds(k, 1), :].rearrange("p k s -> p (k s)"), engines=(PE_ENGINE,), min_val=0,
                        max_val=(NB - 1) * 3 * Q, skip_runtime_bounds_check_because="the block was clamped to NB - 1")
                    for s in range(SB):
                        mm = nc.tensor.matmul(bank[6 + u][:, s * 3 * Q:(s + 1) * 3 * Q], hot_t[:, u, s * P:(s + 1) * P],
                                              q_parts[:, bass.ds(at[s], 3 * Q)], start=True, stop=True)
                    mm.then_inc(qd_done, 1)

                def body(k, n, u, after):
                    pe.wait_ge(hot_ready, k + 1)
                    for s in range(SB):
                        if s == 4 and after >= 2:
                            q_of_destinations(k + 2, u)
                        pe.wait_ge(msg_ready, n + (s + 1))
                        pe.wait_ge(added, n + (s + 1))
                        nc.tensor.matmul(bank[s % 4][:, 0:MW], hot[:, u, s, :], msg[:, u, s, :],
                                         start=True, stop=True).then_inc(product, 1)

                pe.sem_inc(qd_done, UN)
                q_of_destinations(0, 0)
                q_of_destinations(1, 1)
                batches(pe, body)

            @block.scalar
            def _(act):
                def indices(k, u):
                    nc.scalar.copy(index[:, u, :], src_step[:, bass.ds(k, 1), :].rearrange("p k s -> p (k s)")).then_inc(index_ready, 1)

                def body(k, n, u, after):
                    act.wait_ge(weights_ready, k + 1 + UN)
                    act.wait_ge(gathered[u], (k - u) * (16 * SB // UN) + 16 * SB)
                    for s in range(SB):
                        nc.scalar.activation(msg[:, u, s, 0:D], rowsv[:, u, s, 0:D], ACT.Copy,
                                             scale=msg[:, u, s, D:D + 1]).then_inc(msg_ready, 1)
                    if after >= 2:
                        act.wait_ge(msg_ready, n + SB)
                        indices(k + 2, u)

                indices(0, 0)
                indices(1, 1)
                nc.scalar.activation(acc[:].rearrange("p (b m) -> p b m", m=MW), iota[:, 0:1].unsqueeze(2).broadcast_to([P, NB, MW]),
                                     ACT.Copy, scale=0.0).then_inc(cleared_b, 1)
                batches(act, body)

            @block.vector
            def _(dve):
                V = nc.vector
                dve.sem_inc(weights_ready, UN)
                dve.sem_inc(added, 4)

                def one_hot_t(k, u):
                    dve.wait_ge(bc_in[u], (k - u) * (16 // UN) + 16)
                    V.tensor_scalar(hot_t[:, u, :], hot_t[:, u, :], lane[:], None, ALU.is_equal).then_inc(hot_t_ready, 1)

                def front(k, u):
                    here = [0]

                    def link(ins):
                        here[0] += 1
                        ins.then_inc(dve_b, 1)
                        dve.wait_ge(dve_b, k * 2 + here[0])

                    dve.wait_ge(qd_done, k + 1 + UN)
                    dve.wait_ge(gathered[u], (k - u) * (16 * SB // UN) + 16 * SB)
                    qq = msg[:, u, :, 0:3 * Q]
                    link(V.tensor_tensor(qq.rearrange("p s (t q) -> p s t q", t=3),
                                         bank[6 + u][:, 0:SB * 3 * Q].rearrange("p (s t q) -> p s t q", s=SB, t=3),
                                         rowsv[:, u, :, D:ROW].unsqueeze(2).broadcast_to([P, SB, 3, Q]), ALU.mult))
                    link(V.tensor_reduce(e_sc[:, u, :], qq, AX.X, ALU.add))
                    V.tensor_scalar(msg[:, u, :, D], e_sc[:, u, :], 0.0, None, ALU.max)
                    V.tensor_scalar(msg[:, u, :, D + 1], e_sc[:, u, :], -1.0, 0.0, ALU.mult, ALU.max).then_inc(weights_ready, 1)

                def one_hot(k, u):
                    V.tensor_tensor(hot[:, u], iota[:].unsqueeze(1).broadcast_to([P, SB, P]),
                                    dst_step[:, bass.ds(k, 1), :].rearrange("p k s -> p (k s)").unsqueeze(2).broadcast_to([P, SB, P]),
                                    ALU.is_equal).then_inc(hot_ready, 1)

                def body(k, n, u, after):
                    if after >= 1:
                        front(k + 1, 1 - u)
                        if after >= 2:
                            one_hot_t(k + 2, u)
                        one_hot(k + 1, 1 - u)
                    _, at = nc.values_load_multi_w_load_instructions(
                        acc_at[:, bass.ds(k, 1), :].rearrange("p k s -> p (k s)"), engines=(DVE_ENGINE,), min_val=0,
                        max_val=(NB - 1) * MW, skip_runtime_bounds_check_because="the block was clamped to NB - 1")
                    for s in range(SB):
                        dve.wait_ge(product, n + (s + 1))
                        a = acc[:, bass.ds(at[s], MW)]
                        dve.wait_ge(added, n + (s + 4))
                        V.tensor_tensor(a, a, bank[s % 4][:, 0:MW], ALU.add).then_inc(added, 1)

                one_hot_t(0, 0)
                front(0, 0)
                one_hot_t(1, 1)
                one_hot(0, 0)
                dve.wait_ge(cleared_b, 1)
                batches(dve, body)

        with ExitStack() as pg:
            BG = 7
            assert NB % BG == 0
            src_c = sb(pg, "src_c", [P, 1], I32)
            dst_c = sb(pg, "dst_c", [P, 1], I32)
            dst_l = sb(pg, "dst_l", [P, 1], F32)
            rows_s = sb(pg, "rows_s", [P, ROW], F32)
            rows_d = sb(pg, "rows_d", [P, ROW], F32)
            msg_g = sb(pg, "msg_g", [P, MW], F32)
            prod_g = sb(pg, "prod_g", [P, Q], F32)
            e_g = sb(pg, "e_g", [P, 1], F32)
            hot_g = sb(pg, "hot_g", [P, BG, P], F32)
            g_idx, g_rows, g_used = sem("g_idx"), sem("g_rows"), sem("g_used")
            g_turn, g_dve, g_hot, g_mm = sem("g_turn"), sem("g_dve"), sem("g_hot"), sem("g_mm")
            NGB = NB // BG
            LG = 3 + 2 * NGB

            def tiles(eng, body, before=None):
                value = eng.value_load(many[0:1, 0:1], min_val=0, max_val=1)
                with eng.If(value > 0):
                    if before:
                        before()
                    with eng.Fori(0, NT - 1) as t:
                        body(t, P)
                    body(NT - 1, ETAIL)

            block = pg.enter_context(nc.Block())

            @block.gpsimd
            def _(pool):
                def body(t, ne):
                    pool.wait_ge(g_used, t + 1)
                    pool.sem_inc(g_turn, 1)
                    for a, c in ((src, src_c), (dst, dst_c)):
                        pool.dma_start(c[0:ne, :], a[bass.ds(t * P, ne)].rearrange("(p e) -> p e", e=1)).then_inc(g_idx, 16)
                    pool.wait_ge(g_idx, 32 * t + 32)
                    pool.sem_inc(g_turn, 1)
                    for c, rows_ in ((src_c, rows_s), (dst_c, rows_d)):
                        pool.indirect_dma_start(out=rows_[0:ne, :], out_offset=None, in_=table_ap,
                                                in_offset=bass.IndirectOffsetOnAxis(ap=c[0:ne, :], axis=0)).then_inc(g_rows, 16)

                tiles(pool, body)

            @block.tensor
            def _(pe):
                def body(t, ne):
                    for c in range(NGB):
                        pe.wait_ge(g_hot, t * NGB + c + 1)
                        for j in range(BG):
                            mm = nc.tensor.matmul(bank[j][:, 0:MW], hot_g[0:ne, j, :], msg_g[0:ne, :], start=True, stop=True)
                        mm.then_inc(g_mm, 1)

                tiles(pe, body)

            @block.vector
            def _(dve):
                V = nc.vector
                dve.sem_inc(g_used, 1)

                def body(t, ne):
                    n = [0]

                    def link(ins):
                        n[0] += 1
                        ins.then_inc(g_dve, 1)
                        dve.wait_ge(g_dve, t * LG + n[0] + 1)

                    dve.wait_ge(g_rows, 32 * t + 32)
                    V.tensor_copy(dst_l[0:ne, :], dst_c[0:ne, :])
                    link(V.tensor_tensor(prod_g[0:ne, :], rows_s[0:ne, D:ROW], rows_d[0:ne, D:ROW], ALU.mult))
                    link(V.tensor_reduce(e_g[0:ne, :], prod_g[0:ne, :], AX.X, ALU.add))
                    V.tensor_scalar(msg_g[0:ne, D:D + 1], e_g[0:ne, :], 0.0, None, ALU.max)
                    link(V.tensor_scalar(msg_g[0:ne, D + 1:MW], e_g[0:ne, :], -1.0, 0.0, ALU.mult, ALU.max))
                    link(V.tensor_scalar(msg_g[0:ne, 0:D], rows_s[0:ne, 0:D], msg_g[0:ne, D:D + 1], None, ALU.mult))
                    for c in range(NGB):
                        for j in range(BG):
                            last = V.tensor_scalar(hot_g[0:ne, j, :], iota[0:ne, :], float(j * P), dst_l[0:ne, :], ALU.add, ALU.is_equal)
                        last.then_inc(g_hot, 1)
                        dve.wait_ge(g_mm, t * NGB + c + 1)
                        if c < NGB - 1:
                            link(V.tensor_scalar(dst_l[0:ne, :], dst_l[0:ne, :], -float(BG * P), None, ALU.add))
                        for j in range(BG):
                            a = acc[:, (c * BG + j) * MW:(c * BG + j + 1) * MW]
                            last = V.tensor_tensor(a, a, bank[j][:, 0:MW], ALU.add)
                        link(last)
                    V.memset(e_g[:], 0.0).then_inc(g_used, 1)
                    assert n[0] == LG, (n[0], LG)

                def clear():
                    V.memset(acc[:], 0.0).then_inc(g_dve, 1)
                    dve.wait_ge(g_dve, 1)

                tiles(dve, body, clear)

        graph.close()

        with ExitStack() as pc:
            xg = sb(pc, "xg", [P, GB, D], F32)
            xng = sb(pc, "xng", [P, GB, D], F32)
            xt_f = sb(pc, "xt_f", [P, KC, TOK], F32)
            xh = sb(pc, "xh", [P, 2, KC, TOK], F32R)
            xl = sb(pc, "xl", [P, 2, KC, TOK], F32R)
            h_f = sb(pc, "h_f", [P, 2, 2, TOK], F32)
            h_hi = sb(pc, "h_hi", [P, 2, 2, KC, TOK], F32R)
            h_lo = sb(pc, "h_lo", [P, 2, 2, KC, TOK], F32R)
            NW = 4
            gate_bc = sb(pc, "gate_bc", [P, NW, TOK], F32)
            gate_t = sb(pc, "gate_t", [NE, TOK], F32)
            gate_s = sb(pc, "gate_s", [64 + NE, TOK], F32R)
            y_t = xt_f
            lg = sb(pc, "lg", [P, GB, NE], F32)
            lmax = sb(pc, "lmax", [P, GB], F32)
            lexp = gate = lg
            st3 = sb(pc, "st3", [P, GB, 6], F32)
            mv3 = sb(pc, "mv3", [P, GB, 2], F32)
            var3 = sb(pc, "var3", [P, GB], F32)
            sd3 = sb(pc, "sd3", [P, GB], F32)
            rs3 = sb(pc, "rs3", [P, GB], F32)

            c_in, c_var, c_sd, c_xhat, c_xt, c_xtf = (sem(n) for n in ("c_in", "c_var", "c_sd", "c_xhat", "c_xt", "c_xtf"))
            c_split, c_lg, c_sub, c_exp, c_gate = (sem(n) for n in ("c_split", "c_lg", "c_sub", "c_exp", "c_gate"))
            c_gt, c_gtf, c_gs, c_gout = (sem(n) for n in ("c_gt", "c_gtf", "c_gs", "c_gout"))
            c_bc = [sem(f"c_bc{n}") for n in range(NW)]
            mm_1, mm_2, mm_3 = sem("mm_1"), sem("mm_2"), sem("mm_3")
            relu_1, relu_2, split_1, split_2 = sem("relu_1"), sem("relu_2"), sem("split_1"), sem("split_2")
            turn, c_y, c_yt, c_fin, c_out, dve_c = sem("turn"), sem("c_y"), sem("c_yt"), sem("c_fin"), sem("c_out"), sem("dve_c")
            accv = acc[:].rearrange("p (b w) -> p b w", w=MW)
            C2 = 2 * NW
            ITC = (NG - 4) // 2
            HEAD, REST = (0, 1), tuple(range(2 + 2 * ITC, NG + 1))
            FIN = 3

            def start(g):
                return 0 if isinstance(g, int) and g == 0 else g * GB - 1

            def at_block(g, j):
                return bass.ds(start(g) + j, 1)

            def tokens(g, nb):
                return bass.ds(start(g) * P, nb * P)

            def is_last(g):
                return isinstance(g, int) and g == NG - 1

            def peeled(g):
                size = lambda n: SIZE[n] if 0 <= n < NG else 0
                return g, size(g), g % 2, size(g - 1), size(g + 1)

            def groups(eng, first, body):
                first(0, SIZE[0], 0)
                for g in HEAD:
                    body(*peeled(g))
                with eng.Fori(0, ITC) as it:
                    body(it * 2 + 2, GB, 0, GB, GB)
                    body(it * 2 + 3, GB, 1, GB, GB)
                for g in REST:
                    body(*peeled(g))

            def slots(nb):
                return range(NE if nb else 2)

            def back(g, nb, par, prev, e, by):
                if e >= by:
                    return (g, e - by, nb, par) if nb else None
                return (g - 1, e - by + NE, prev, 1 - par) if prev else None

            def finish_at(nb, prev, e):
                return prev and e == (FIN if nb else 1)

            block = pc.enter_context(nc.Block())

            @block.sync
            def _(sp):
                def load(g, nb, par):
                    rows_g = tokens(g, nb)
                    sp.dma_start(xng[:, 0:nb, :], table_ap[rows_g, 0:D].rearrange("(b p) d -> p b d", p=P)).then_inc(c_in, 16)
                    if is_last(g):
                        sp.dma_start(xg[:, 0, :], x[(NB - 2) * P:(NB - 1) * P, :]).then_inc(c_in, 16)
                        sp.dma_start(xg[0:TAIL, 1, :], x[(NB - 1) * P:N, :]).then_inc(c_in, 16)
                    else:
                        sp.dma_start(xg[:, 0:nb, :], x[rows_g, :].rearrange("(b p) d -> p b d", p=P)).then_inc(c_in, 16)

                def body(g, nb, par, prev, nxt):
                    if nb == 0:
                        return
                    if nxt:
                        sp.wait_ge(c_xt, g + 1)
                        load(g + 1, nxt, 1 - par)
                    sp.wait_ge(c_gout, 16 * (g + 1))
                    sp.sem_inc(turn, 1)
                    for e in range(NE):
                        sp.wait_ge(split_2, g * 16 + 2 * e + 2)
                        sp.sem_inc(turn, 1)
                        sp.dma_start(gate_bc[:, e % NW, 0:nb * P], gates_ap[e:e + 1, tokens(g, nb)].rearrange("a n -> (a n)").partition_broadcast(P)
                                     ).then_inc(c_bc[e % NW], 16)

                groups(sp, load, body)

            @block.gpsimd
            def _(pool):
                def gates_out(g, nb, par):
                    pool.wait_ge(c_gtf, g + 1)
                    pool.dma_start(gates_ap[:, tokens(g, nb)], gate_t[:, 0:nb * P]).then_inc(c_gout, 16)

                def body(g, nb, par, prev, nxt):
                    if prev:
                        pool.wait_ge(c_fin, g + 2)
                        if is_last(g - 1):
                            pool.dma_start(out[(NB - 2) * P:(NB - 1) * P, :], accv[:, NB - 2, 0:D]).then_inc(c_out, 16)
                            pool.dma_start(out[(NB - 1) * P:N, :], accv[0:TAIL, NB - 1, 0:D]).then_inc(c_out, 16)
                        else:
                            pool.dma_start(out[tokens(g - 1, prev), :].rearrange("(b p) d -> p b d", p=P),
                                           accv[:, bass.ds(start(g - 1), prev), 0:D]).then_inc(c_out, 16)
                    if nxt:
                        gates_out(g + 1, nxt, 1 - par)

                groups(pool, gates_out, body)
                pool.wait_ge(c_out, 16 * (NG + 1))
                pool.wait_ge(c_gout, 16 * NG)

            @block.tensor
            def _(pe):
                M = nc.tensor.matmul
                pe.sem_inc(mm_3, 2)
                pe.sem_inc(c_yt, 1)

                def turn(g, nb, par):
                    pe.wait_ge(c_xhat, g + 1)
                    pe.wait_ge(c_fin, g + 1)
                    for k in range(KC):
                        for j in range(nb):
                            mm = nc.tensor.transpose(bank[6 + k][:, j * P:(j + 1) * P], xg[:, j, k * P:(k + 1) * P], ident[:])
                    mm.then_inc(c_xt, 1)

                def logits(g, nb, par):
                    pe.wait_ge(c_xtf, 2 * (g + 1))
                    for j in range(nb):
                        for k in range(KC):
                            mm = M(bank[6][:, j * NE:(j + 1) * NE], xt_f[:, k, j * P:(j + 1) * P], wr_sb[:, k, :],
                                   start=(k == 0), stop=(k == KC - 1))
                    mm.then_inc(c_lg, 1)

                def turn_gates(g, nb, par):
                    pe.wait_ge(c_gate, g + 1)
                    for j in range(nb):
                        mm = nc.tensor.transpose(bank[7][0:NE, j * P:(j + 1) * P], gate[:, j, :], ident[:])
                    mm.then_inc(c_gt, 1)

                def three(out_, n, k, m, hi, lo, first, last):
                    a, b = wh[:, n, k * D + m * P:k * D + (m + 1) * P], wl[:, n, k * D + m * P:k * D + (m + 1) * P]
                    M(out_, a, hi, start=first, stop=False)
                    M(out_, a, lo, start=False, stop=False)
                    return M(out_, b, hi, start=False, stop=last)

                def layer_1(g, e, nb, par):
                    T = nb * P
                    if e == 0:
                        pe.wait_ge(c_split, g + 1)
                    for m in range(2):
                        pe.wait_ge(relu_1, g * 16 + e * 2 + m + 1)
                        for k in range(KC):
                            mm = three(bank[m][:, 0:T], e, k, m, xh[:, par, k, 0:T], xl[:, par, k, 0:T], k == 0, k == KC - 1)
                        mm.then_inc(mm_1, 1)

                def layer_2(g, e, nb, par):
                    T = nb * P
                    pe.wait_ge(split_1, g * 16 + e * 2 + 2 + 2)
                    for m in range(2):
                        pe.wait_ge(relu_2, g * 16 + e * 2 + m + 1)
                        for k in range(KC):
                            mm = three(bank[2 + m][:, 0:T], NE + e, k, m, h_hi[:, 0, e % 2, k, 0:T], h_lo[:, 0, e % 2, k, 0:T], k == 0, k == KC - 1)
                        mm.then_inc(mm_2, 1)

                def layer_3(g, e, nb, par):
                    T = nb * P
                    if e == 0:
                        pe.wait_ge(c_gs, g + 1)
                        pe.wait_ge(c_y, 2 * g + 2)
                        for m in range(KC):
                            M(bank[4 + m][:, 0:T], bo_s[:, m * P:(m + 1) * P], gate_s[:, 0:T], start=True, stop=False)
                    pe.wait_ge(split_2, g * 16 + e * 2 + 2 + C2)
                    for m in range(KC):
                        for k in range(KC):
                            mm = three(bank[4 + m][:, 0:T], 2 * NE + e, k, m, h_hi[:, 1, e % 2, k, 0:T], h_lo[:, 1, e % 2, k, 0:T],
                                       False, e == NE - 1 and k == KC - 1)
                    mm.then_inc(mm_3, 1)

                def turn_back(g, nb, more):
                    pe.wait_ge(c_y, 2 * g + 4)
                    if more:
                        pe.wait_ge(c_gtf, g + 2)
                    for j in range(nb):
                        for m in range(KC):
                            mm = nc.tensor.transpose(bank[6 + j // 2][:, (j % 2 * KC + m) * P:(j % 2 * KC + m + 1) * P],
                                                     y_t[:, m, j * P:(j + 1) * P], ident[:])
                    mm.then_inc(c_yt, 1)

                def body(g, nb, par, prev, nxt):
                    for e in slots(nb):
                        for by, layer in enumerate((layer_1, layer_2, layer_3)):
                            it_is = back(g, nb, par, prev, e, by)
                            if it_is:
                                layer(*it_is)
                        if finish_at(nb, prev, e):
                            turn_back(g - 1, prev, nb)
                        if nxt and e == 4:
                            turn(g + 1, nxt, 1 - par)
                        if nxt and e == 5:
                            logits(g + 1, nxt, 1 - par)
                        if nxt and e == 7:
                            turn_gates(g + 1, nxt, 1 - par)

                def first(g, nb, par):
                    turn(g, nb, par)
                    logits(g, nb, par)
                    turn_gates(g, nb, par)

                groups(pe, first, body)

            @block.scalar
            def _(act):
                A = nc.scalar.activation
                act.sem_inc(relu_1, 2)
                act.sem_inc(relu_2, 2)
                act.sem_inc(c_y, 2)

                def norm(g, nb, par):
                    act.wait_ge(c_var, g + 1)
                    A(sd3[:, 0:nb], var3[:, 0:nb], ACT.Sqrt).then_inc(c_sd, 1)

                def turned(g, nb, par):
                    act.wait_ge(c_xt, g + 1)
                    for k in range(KC):
                        nc.scalar.copy(xt_f[:, k, 0:nb * P], bank[6 + k][:, 0:nb * P]).then_inc(c_xtf, 1)

                def exps(g, nb, par):
                    act.wait_ge(c_sub, g + 1)
                    A(lexp[:, 0:nb, :], lg[:, 0:nb, :], ACT.Exp).then_inc(c_exp, 1)

                def gates(g, nb, par):
                    act.wait_ge(c_gt, g + 1)
                    if not (isinstance(g, int) and g == 0):
                        act.wait_ge(c_gout, 16 * g)
                    nc.scalar.copy(gate_t[:, 0:nb * P], bank[7][0:NE, 0:nb * P]).then_inc(c_gtf, 1)

                def relu(layer, g, e, nb, mm, ready, split, more):
                    for m in range(2):
                        n = g * 16 + e * 2 + m + 1
                        act.wait_ge(mm, n)
                        act.wait_ge(split, n + more)
                        A(h_f[:, layer, m, 0:nb * P], bank[2 * layer + m][:, 0:nb * P], ACT.Relu,
                          bias=bn_c[:, layer, 2 * e + m:2 * e + m + 1], scale=bn_s[:, layer, 2 * e + m:2 * e + m + 1]).then_inc(ready, 1)

                def results(g, nb):
                    act.wait_ge(mm_3, (g + 1) * NE + 2)
                    act.wait_ge(c_yt, g + 1)
                    for m in range(KC):
                        nc.scalar.copy(y_t[:, m, 0:nb * P], bank[4 + m][:, 0:nb * P]).then_inc(c_y, 1)

                def body(g, nb, par, prev, nxt):
                    for e in slots(nb):
                        if nb:
                            relu(0, g, e, nb, mm_1, relu_1, split_1, 0)
                        before = back(g, nb, par, prev, e, 1)
                        if before:
                            relu(1, *before[:3], mm_2, relu_2, split_2, C2 - 2)
                        if prev and e == 1:
                            results(g - 1, prev)
                        if nxt and e == 2:
                            norm(g + 1, nxt, 1 - par)
                        if nxt and e == 4:
                            turned(g + 1, nxt, 1 - par)
                        if nxt and e == 6:
                            exps(g + 1, nxt, 1 - par)
                        if nxt and e == 7:
                            gates(g + 1, nxt, 1 - par)

                def first(g, nb, par):
                    norm(g, nb, par)
                    turned(g, nb, par)
                    exps(g, nb, par)
                    gates(g, nb, par)

                groups(act, first, body)

            @block.vector
            def _(dve):
                V = nc.vector
                base = [None, 0, 0]

                def link(ins):
                    base[1] += 1
                    ins.then_inc(dve_c, 1)
                    dve.wait_ge(dve_c, base[0] + base[1])

                dve.sem_inc(split_1, 2)
                dve.sem_inc(split_2, C2)
                dve.sem_inc(c_fin, 2)
                base[0] = 0
                link(V.memset(gate_s[:].bitcast(F32), 0.0))
                a_sum, r_sum = accv[:, :, D], accv[:, :, D + 1]
                link(V.tensor_tensor(a_sum, a_sum, r_sum, ALU.add))
                link(V.tensor_scalar(a_sum, a_sum, DEN_EPS, None, ALU.add))
                link(V.reciprocal(a_sum, a_sum))
                link(V.tensor_tensor(r_sum, r_sum, a_sum, ALU.mult))

                def residual(g, nb, par, stage):
                    a = [accv[:, at_block(g, j), 0:D].rearrange("p b d -> p (b d)") for j in range(nb)]
                    column = lambda j, c: accv[:, at_block(g, j), c:c + 1].rearrange("p b d -> p (b d)")
                    if stage == 0:
                        dve.wait_ge(c_in, 32 * (g + 1) + (16 if is_last(g) else 0))
                        for j in range(nb):
                            last = V.scalar_tensor_tensor(out=a[j], in0=a[j], scalar=column(j, D), in1=xg[:, j, :], op0=ALU.mult, op1=ALU.add)
                        link(last)
                    if stage == 1:
                        for j in range(nb):
                            last = V.scalar_tensor_tensor(out=a[j], in0=xng[:, j, :], scalar=column(j, D + 1), in1=a[j], op0=ALU.mult, op1=ALU.add)
                        link(last)
                        V.memset(var3[:, 0:1], 0.0)
                    if stage == 2:
                        for j in range(nb):
                            last = V.bn_stats(st3[:, j, :], a[j])
                        link(last)
                        V.memset(var3[:, 0:1], 0.0)
                        for j in range(nb):
                            last = V.bn_aggr(mv3[:, j, :], st3[:, j, :])
                        link(last)
                        V.tensor_scalar(var3[:, 0:nb], mv3[:, 0:nb, 1], LN_EPS, None, ALU.add).then_inc(c_var, 1)

                def norm(g, nb, par):
                    dve.wait_ge(c_sd, g + 1)
                    link(V.reciprocal(rs3[:, 0:nb], sd3[:, 0:nb]))
                    for j in range(nb):
                        last = V.tensor_scalar(xg[:, j, :], accv[:, at_block(g, j), 0:D].rearrange("p b d -> p (b d)"),
                                               mv3[:, j, 0:1], rs3[:, j:j + 1], ALU.subtract, ALU.mult)
                    last.then_inc(c_xhat, 1)

                def split_x(g, nb, par):
                    dve.wait_ge(c_xtf, 2 * (g + 1))
                    T = nb * P
                    link(V.tensor_copy(xh[:, par, :, 0:T], xt_f[:, :, 0:T]))
                    V.tensor_tensor(xl[:, par, :, 0:T], xt_f[:, :, 0:T], xh[:, par, :, 0:T].bitcast(F32), ALU.subtract).then_inc(c_split, 1)

                def softmax_1(g, nb, par):
                    dve.wait_ge(c_lg, g + 1)
                    l = lg[:, 0:nb, :]
                    link(V.tensor_tensor(l, bank[6][:, 0:nb * NE].rearrange("p (b e) -> p b e", e=NE),
                                         br_sb[:].unsqueeze(1).broadcast_to([P, nb, NE]), ALU.add))
                    link(V.tensor_reduce(lmax[:, 0:nb], l, AX.X, ALU.max))
                    V.tensor_tensor(l, l, lmax[:, 0:nb].unsqueeze(2).broadcast_to([P, nb, NE]), ALU.subtract).then_inc(c_sub, 1)

                def softmax_2(g, nb, par):
                    dve.wait_ge(c_exp, g + 1)
                    link(V.tensor_reduce(lmax[:, 0:nb], lexp[:, 0:nb, :], AX.X, ALU.add))
                    link(V.reciprocal(lmax[:, 0:nb], lmax[:, 0:nb]))
                    V.tensor_tensor(gate[:, 0:nb, :], lexp[:, 0:nb, :], lmax[:, 0:nb].unsqueeze(2).broadcast_to([P, nb, NE]), ALU.mult).then_inc(c_gate, 1)

                def split_relu_1(g, e, nb):
                    T = nb * P
                    for m in range(2):
                        dve.wait_ge(relu_1, g * 16 + e * 2 + m + 3)
                        hi = h_hi[:, 0, e % 2, m, 0:T]
                        link(V.tensor_copy(hi, h_f[:, 0, m, 0:T]))
                        V.tensor_tensor(h_lo[:, 0, e % 2, m, 0:T], h_f[:, 0, m, 0:T], hi.bitcast(F32), ALU.subtract).then_inc(split_1, 1)

                def split_relu_2(g, e, nb):
                    T = nb * P
                    for m in range(2):
                        dve.wait_ge(relu_2, g * 16 + e * 2 + m + 3)
                        if m == 0:
                            dve.wait_ge(c_bc[e % NW], (g * 2 + e // NW + 1) * 16)
                            dve.wait_ge(mm_3, g * NE + e + 1)
                        link(V.tensor_tensor(h_f[:, 1, m, 0:T], h_f[:, 1, m, 0:T], gate_bc[:, e % NW, 0:T], ALU.mult))
                        hi = h_hi[:, 1, e % 2, m, 0:T]
                        link(V.tensor_copy(hi, h_f[:, 1, m, 0:T]))
                        V.tensor_tensor(h_lo[:, 1, e % 2, m, 0:T], h_f[:, 1, m, 0:T], hi.bitcast(F32), ALU.subtract).then_inc(split_2, 1)

                def split_gates(g, nb):
                    T = nb * P
                    dve.wait_ge(c_gtf, g + 1)
                    link(V.tensor_copy(gate_s[0:NE, 0:T], gate_t[:, 0:T]))
                    V.tensor_tensor(gate_s[32:32 + NE, 0:T], gate_t[:, 0:T], gate_s[0:NE, 0:T].bitcast(F32), ALU.subtract)
                    V.tensor_copy(gate_s[64:64 + NE, 0:T], gate_s[0:NE, 0:T].bitcast(F32)).then_inc(c_gs, 1)

                def finish(g, nb):
                    dve.wait_ge(c_yt, g + 2)
                    for j in range(nb):
                        a = accv[:, at_block(g, j), 0:D].rearrange("p b d -> p (b d)")
                        last = V.tensor_tensor(a, a, bank[6 + j // 2][:, j % 2 * D:(j % 2 + 1) * D], ALU.add)
                    last.then_inc(c_fin, 1)

                def body(g, nb, par, prev, nxt):
                    for e in slots(nb):
                        if nb:
                            split_relu_1(g, e, nb)
                        if nxt and e == 7:
                            softmax_2(g + 1, nxt, 1 - par)
                        before = back(g, nb, par, prev, e, 1)
                        if before:
                            split_relu_2(*before[:3])
                        if nb and e == 1:
                            split_gates(g, nb)
                        if finish_at(nb, prev, e):
                            finish(g - 1, prev)
                        if nxt and e < 3:
                            residual(g + 1, nxt, 1 - par, e)
                        if nxt and e == 3:
                            norm(g + 1, nxt, 1 - par)
                        if nxt and e == 5:
                            split_x(g + 1, nxt, 1 - par)
                        if nxt and e == 6:
                            softmax_1(g + 1, nxt, 1 - par)

                for stage in range(3):
                    residual(0, SIZE[0], 0, stage)
                norm(0, SIZE[0], 0)
                split_x(0, SIZE[0], 0)
                softmax_1(0, SIZE[0], 0)
                softmax_2(0, SIZE[0], 0)
                LINKS = 4 + 1 + 1 + 2 + 2 + 1 + 2 * NE + 4 * NE
                for g in HEAD:
                    body(*peeled(g))
                ahead = base[1]
                with dve.Fori(0, ITC) as it:
                    base[0], base[1] = it * (2 * LINKS) + ahead, 0
                    body(it * 2 + 2, GB, 0, GB, GB)
                    body(it * 2 + 3, GB, 1, GB, GB)
                    assert base[1] == 2 * LINKS, base[1]
                base[0], base[1] = ahead + ITC * 2 * LINKS, 0
                for g in REST:
                    body(*peeled(g))


_BN1 = ["L0_ffn_b1", "L0_ffn_g1", "L0_ffn_be1", "L0_ffn_m1", "L0_ffn_v1"]
_BN2 = ["L0_ffn_b2", "L0_ffn_g2", "L0_ffn_be2", "L0_ffn_m2", "L0_ffn_v2"]
_INS = ["x", "src", "dst", "L0_gnn_W_dis", "L0_ffn_Wr", "L0_ffn_br", *_BN1, *_BN2, "L0_ffn_W1", "L0_ffn_W2", "L0_ffn_Wo", "L0_ffn_bo"]


def kernel(**inputs):
    import numpy as np
    import concourse.bacc as bacc
    from concourse import mybir as mb
    from concourse.bass_utils import run_bass_kernel_spmd

    nc = bacc.Bacc("TRN2", target_bir_lowering=False, num_devices=1)
    arrays, a = {}, {}
    for name in _INS:
        v = np.ascontiguousarray(inputs[name])
        arrays[f"in_{name}"] = v
        a[name] = nc.dram_tensor(f"in_{name}", v.shape, mb.dt.from_np(v.dtype), kind="ExternalInput").ap()
    out = nc.dram_tensor("out", arrays["in_x"].shape, mb.dt.float32, kind="ExternalOutput").ap()
    graph_mixture(nc, a["x"], a["src"], a["dst"], a["L0_gnn_W_dis"], a["L0_ffn_Wr"], a["L0_ffn_br"],
                  [a[n] for n in _BN1], [a[n] for n in _BN2], a["L0_ffn_W1"], a["L0_ffn_W2"], a["L0_ffn_Wo"], a["L0_ffn_bo"], out)
    r = run_bass_kernel_spmd(nc, [arrays], core_ids=[0])
    return r.results[0]["out"]
```
